# Optimizing a Trainium2 kernel written in Bass

```python
import numpy as np
import jax
import jax.numpy as jnp

def _softmax(x, axis=-1):
    return jax.nn.softmax(x, axis=axis)

def _gelu(x):
    return jax.nn.gelu(x, approximate=True)

def _silu(x):
    return jax.nn.silu(x)

def _sigmoid(x):
    return jax.nn.sigmoid(x)

def _layernorm(x, axis=-1, eps=1e-05):
    m = jnp.mean(x, axis=axis, keepdims=True)
    v = jnp.var(x, axis=axis, keepdims=True)
    return (x - m) / jnp.sqrt(v + eps)

def _scatter_add(tgt, idx, src, axis=0):
    return tgt.at[idx].add(src)

def _segment_sum(src, seg, n):
    return jax.ops.segment_sum(src, seg, n)
kernel_name = 'mk_gnn_preln_d4_gnn_r32_641c8f'

def setup_inputs(seed: int=0):
    np.random.seed(seed)
    _w = jnp.asarray

    def _rec_inputs():
        import jax
        import jax.numpy as jnp
        _gk = jax.random.key(seed)
        x = -0.0001006 + 1 * jax.random.normal(jax.random.fold_in(_gk, 1), (3125, 96), jnp.float32)
        src = jax.random.randint(jax.random.fold_in(_gk, 2), (100000,), 0, 3125, jnp.int32)
        dst = jax.random.randint(jax.random.fold_in(_gk, 3), (100000,), 0, 3125, jnp.int32)
        _o = jnp.argsort(dst, stable=True)
        src = src[_o]
        dst = dst[_o]
        edge_attr_32 = 0.000196303 + 1.00016 * jax.random.normal(jax.random.fold_in(_gk, 12), (100000, 32), jnp.float32)
        edge_attr_96 = -4.21973e-06 + 0.0999841 * jax.random.normal(jax.random.fold_in(_gk, 13), (100000, 96), jnp.float32)
        edge_weight = jax.random.uniform(jax.random.fold_in(_gk, 15), (100000,), jnp.float32, 0.0, 0.999998)
        return (x, src, dst, edge_attr_32, edge_attr_96, edge_weight)
    x, src, dst, edge_attr_32, edge_attr_96, edge_weight = _rec_inputs()

    def _L0_gnn_setup():
        import jax, jax.numpy as jnp
        import numpy as np
        LN_EPS = 1e-05
        N_NODES = 50000
        N_EDGES = 25000
        IN_DIM = 96
        OUT_DIM = 96
        key = jax.random.key(seed)
        k = jax.random.split(key, 5)
        x = jax.random.normal(k[0], (N_NODES, IN_DIM), dtype=jnp.float32)
        edge_index = jax.random.randint(k[1], (2, N_EDGES), 0, N_NODES, dtype=jnp.int64 if jax.config.read('jax_enable_x64') else jnp.int32)
        edge_weight = jax.random.uniform(k[2], (N_EDGES,), dtype=jnp.float32)
        W = jax.random.normal(k[3], (IN_DIM, OUT_DIM), dtype=jnp.float32) / np.sqrt(IN_DIM)
        bias = jnp.zeros((OUT_DIM,), dtype=jnp.float32)
        gamma = jnp.ones((OUT_DIM,), dtype=jnp.float32)
        beta = jnp.zeros((OUT_DIM,), dtype=jnp.float32)
        return {'x': x, 'edge_index': edge_index, 'edge_weight': edge_weight, 'W': W, 'bias': bias, 'gamma': gamma, 'beta': beta}
    _L0_gnn_all = _L0_gnn_setup()
    _L0_gnn_in = {k: v for k, v in _L0_gnn_all.items() if k in ('W', 'bias', 'gamma', 'beta')}
    del _L0_gnn_all

    def _L1_gnn_setup():
        import jax, jax.numpy as jnp
        import numpy as np
        N_NODES = 50000
        N_EDGES = 25000
        D = 96
        LN_EPS = 1e-05

        def _layer(h, src, dst, norm, n_nodes, W, b, g, be):
            h = h @ W
            msg = h[src] * norm[:, None]
            h = jax.ops.segment_sum(msg, dst, num_segments=n_nodes) + b
            h = jnp.tanh(h)
            mu = jnp.mean(h, axis=-1, keepdims=True)
            var = jnp.mean(jnp.square(h - mu), axis=-1, keepdims=True)
            h = (h - mu) * jax.lax.rsqrt(var + LN_EPS)
            return h * g + be
        key = jax.random.key(seed)
        ks = jax.random.split(key, 4)
        x = jax.random.normal(ks[0], (N_NODES, D), dtype=jnp.float32)
        edge_index = jax.random.randint(ks[1], (2, N_EDGES), 0, N_NODES, dtype=jnp.int64)
        scale = 1.0 / np.sqrt(D)
        W0 = jax.random.normal(ks[2], (D, D), dtype=jnp.float32) * scale
        W1 = jax.random.normal(ks[3], (D, D), dtype=jnp.float32) * scale
        b0 = jnp.zeros((D,), jnp.float32)
        b1 = jnp.zeros((D,), jnp.float32)
        g0 = jnp.ones((D,), jnp.float32)
        g1 = jnp.ones((D,), jnp.float32)
        be0 = jnp.zeros((D,), jnp.float32)
        be1 = jnp.zeros((D,), jnp.float32)
        return {'x': x, 'edge_index': edge_index, 'W0': W0, 'b0': b0, 'g0': g0, 'be0': be0, 'W1': W1, 'b1': b1, 'g1': g1, 'be1': be1}
    _L1_gnn_all = _L1_gnn_setup()
    _L1_gnn_in = {k: v for k, v in _L1_gnn_all.items() if k in ('W0', 'b0', 'g0', 'be0', 'W1', 'b1', 'g1', 'be1')}
    del _L1_gnn_all

    def _L2_gnn_setup():
        import jax, jax.numpy as jnp
        import numpy as np
        N, E = (50000, 25000)
        ND, ED = (96, 32)

        def _gelu(x):
            return jax.nn.gelu(x, approximate=False)
        key = jax.random.key(seed)
        ks = jax.random.split(key, 16)
        s = lambda fan_in: 1.0 / np.sqrt(fan_in)
        inp = {'x': jax.random.normal(ks[0], (N, ND), jnp.float32), 'edge_index': jax.random.randint(ks[1], (2, E), 0, N, jnp.int32), 'edge_attr': jax.random.normal(ks[2], (E, ED), jnp.float32), 'mW1': jax.random.uniform(ks[3], (ND + ED, ND), jnp.float32, -s(ND + ED), s(ND + ED)), 'mb1': jnp.zeros((ND,), jnp.float32), 'mW2': jax.random.uniform(ks[4], (ND, ND), jnp.float32, -s(ND), s(ND)), 'mb2': jnp.zeros((ND,), jnp.float32), 'gW1': jax.random.uniform(ks[5], (ND + ED, ND), jnp.float32, -s(ND + ED), s(ND + ED)), 'gb1': jnp.zeros((ND,), jnp.float32), 'gW2': jax.random.uniform(ks[6], (ND, 1), jnp.float32, -s(ND), s(ND)), 'gb2': jnp.zeros((1,), jnp.float32), 'uW1': jax.random.uniform(ks[7], (2 * ND, ND), jnp.float32, -s(2 * ND), s(2 * ND)), 'ub1': jnp.zeros((ND,), jnp.float32), 'uW2': jax.random.uniform(ks[8], (ND, ND), jnp.float32, -s(ND), s(ND)), 'ub2': jnp.zeros((ND,), jnp.float32), 'ln_g': jnp.ones((ND,), jnp.float32), 'ln_b': jnp.zeros((ND,), jnp.float32)}
        return inp
    _L2_gnn_all = _L2_gnn_setup()
    _L2_gnn_in = {k: v for k, v in _L2_gnn_all.items() if k in ('mW1', 'mb1', 'mW2', 'mb2', 'gW1', 'gb1', 'gW2', 'gb2', 'uW1', 'ub1', 'uW2', 'ub2', 'ln_g', 'ln_b')}
    del _L2_gnn_all

    def _L3_gnn_setup():
        import jax, jax.numpy as jnp
        import numpy as np
        N_NODES = 50000
        N_EDGES = 25000
        HID = 96

        def _gelu(x):
            return jax.nn.gelu(x, approximate=False)
        key = jax.random.key(seed)
        ks = jax.random.split(key, 12)
        s = 1.0 / np.sqrt(HID)
        return {'x_feat': jax.random.normal(ks[0], (N_NODES, HID), jnp.float32), 'bases': jax.random.normal(ks[1], (N_EDGES, HID), jnp.float32) * 0.1, 'W_pre': jax.random.normal(ks[2], (HID, HID), jnp.float32) * s, 'b_pre': jax.random.normal(ks[3], (HID,), jnp.float32) * s, 'W1': jax.random.normal(ks[4], (HID, HID), jnp.float32) * s, 'b1': jax.random.normal(ks[5], (HID,), jnp.float32) * s, 'W2': jax.random.normal(ks[6], (HID, HID), jnp.float32) * s, 'b2': jax.random.normal(ks[7], (HID,), jnp.float32) * s, 'src': jax.random.randint(ks[8], (N_EDGES,), 0, N_NODES, jnp.int32), 'dst': jax.random.randint(ks[9], (N_EDGES,), 0, N_NODES, jnp.int32)}
    _L3_gnn_all = _L3_gnn_setup()
    _L3_gnn_in = {k: v for k, v in _L3_gnn_all.items() if k in ('W_pre', 'b_pre', 'W1', 'b1', 'W2', 'b2')}
    del _L3_gnn_all
    return {'x': x, 'src': src, 'dst': dst, 'edge_attr_32': edge_attr_32, 'edge_attr_96': edge_attr_96, 'edge_weight': edge_weight, 'L0_gnn_W': _L0_gnn_in['W'], 'L0_gnn_bias': _L0_gnn_in['bias'], 'L0_gnn_gamma': _L0_gnn_in['gamma'], 'L0_gnn_beta': _L0_gnn_in['beta'], 'L1_gnn_W0': _L1_gnn_in['W0'], 'L1_gnn_b0': _L1_gnn_in['b0'], 'L1_gnn_g0': _L1_gnn_in['g0'], 'L1_gnn_be0': _L1_gnn_in['be0'], 'L1_gnn_W1': _L1_gnn_in['W1'], 'L1_gnn_b1': _L1_gnn_in['b1'], 'L1_gnn_g1': _L1_gnn_in['g1'], 'L1_gnn_be1': _L1_gnn_in['be1'], 'L2_gnn_mW1': _L2_gnn_in['mW1'], 'L2_gnn_mb1': _L2_gnn_in['mb1'], 'L2_gnn_mW2': _L2_gnn_in['mW2'], 'L2_gnn_mb2': _L2_gnn_in['mb2'], 'L2_gnn_gW1': _L2_gnn_in['gW1'], 'L2_gnn_gb1': _L2_gnn_in['gb1'], 'L2_gnn_gW2': _L2_gnn_in['gW2'], 'L2_gnn_gb2': _L2_gnn_in['gb2'], 'L2_gnn_uW1': _L2_gnn_in['uW1'], 'L2_gnn_ub1': _L2_gnn_in['ub1'], 'L2_gnn_uW2': _L2_gnn_in['uW2'], 'L2_gnn_ub2': _L2_gnn_in['ub2'], 'L2_gnn_ln_g': _L2_gnn_in['ln_g'], 'L2_gnn_ln_b': _L2_gnn_in['ln_b'], 'L3_gnn_W_pre': _L3_gnn_in['W_pre'], 'L3_gnn_b_pre': _L3_gnn_in['b_pre'], 'L3_gnn_W1': _L3_gnn_in['W1'], 'L3_gnn_b1': _L3_gnn_in['b1'], 'L3_gnn_W2': _L3_gnn_in['W2'], 'L3_gnn_b2': _L3_gnn_in['b2']}

def reference(x, src, dst, edge_attr_32, edge_attr_96, edge_weight, L0_gnn_W, L0_gnn_bias, L0_gnn_gamma, L0_gnn_beta, L1_gnn_W0, L1_gnn_b0, L1_gnn_g0, L1_gnn_be0, L1_gnn_W1, L1_gnn_b1, L1_gnn_g1, L1_gnn_be1, L2_gnn_mW1, L2_gnn_mb1, L2_gnn_mW2, L2_gnn_mb2, L2_gnn_gW1, L2_gnn_gb1, L2_gnn_gW2, L2_gnn_gb2, L2_gnn_uW1, L2_gnn_ub1, L2_gnn_uW2, L2_gnn_ub2, L2_gnn_ln_g, L2_gnn_ln_b, L3_gnn_W_pre, L3_gnn_b_pre, L3_gnn_W1, L3_gnn_b1, L3_gnn_W2, L3_gnn_b2):
    import jax
    import jax.numpy as jnp

    def _L0_gnn_ref(x, edge_index, edge_weight, W, bias, gamma, beta):
        import jax, jax.numpy as jnp
        import numpy as np
        LN_EPS = 1e-05
        N_NODES = 50000
        N_EDGES = 25000
        IN_DIM = 96
        OUT_DIM = 96
        h = x @ W
        src, dst = (edge_index[0], edge_index[1])
        msgs = h[src] * edge_weight[:, None]
        agg = jax.ops.segment_sum(msgs, dst, num_segments=x.shape[0])
        y = agg + bias
        mu = jnp.mean(y, axis=-1, keepdims=True)
        var = jnp.mean(jnp.square(y - mu), axis=-1, keepdims=True)
        y = (y - mu) * jax.lax.rsqrt(var + LN_EPS)
        return y * gamma + beta

    def _L1_gnn_ref(x, edge_index, W0, b0, g0, be0, W1, b1, g1, be1):
        import jax, jax.numpy as jnp
        import numpy as np
        N_NODES = 50000
        N_EDGES = 25000
        D = 96
        LN_EPS = 1e-05

        def _layer(h, src, dst, norm, n_nodes, W, b, g, be):
            h = h @ W
            msg = h[src] * norm[:, None]
            h = jax.ops.segment_sum(msg, dst, num_segments=n_nodes) + b
            h = jnp.tanh(h)
            mu = jnp.mean(h, axis=-1, keepdims=True)
            var = jnp.mean(jnp.square(h - mu), axis=-1, keepdims=True)
            h = (h - mu) * jax.lax.rsqrt(var + LN_EPS)
            return h * g + be
        n = x.shape[0]
        loops = jnp.arange(n, dtype=edge_index.dtype)
        src = jnp.concatenate([edge_index[0], loops])
        dst = jnp.concatenate([edge_index[1], loops])
        deg = jax.ops.segment_sum(jnp.ones(src.shape, x.dtype), dst, num_segments=n)
        dis = jax.lax.rsqrt(deg)
        norm = dis[src] * dis[dst]
        h = _layer(x, src, dst, norm, n, W0, b0, g0, be0)
        h = _layer(h, src, dst, norm, n, W1, b1, g1, be1)
        return h

    def _L2_gnn_ref(x, edge_index, edge_attr, mW1, mb1, mW2, mb2, gW1, gb1, gW2, gb2, uW1, ub1, uW2, ub2, ln_g, ln_b):
        import jax, jax.numpy as jnp
        import numpy as np
        N, E = (50000, 25000)
        ND, ED = (96, 32)

        def _gelu(x):
            return jax.nn.gelu(x, approximate=False)
        src, dst = (edge_index[0], edge_index[1])
        edge_input = jnp.concatenate([x[src], edge_attr], axis=-1)
        messages = _gelu(edge_input @ mW1 + mb1) @ mW2 + mb2
        gates = jax.nn.sigmoid(_gelu(edge_input @ gW1 + gb1) @ gW2 + gb2)
        aggregated = jax.ops.segment_sum(messages * gates, dst, num_segments=x.shape[0])
        combined = jnp.concatenate([x, aggregated], axis=-1)
        update = _gelu(combined @ uW1 + ub1) @ uW2 + ub2
        h = x + update
        mu = jnp.mean(h, axis=-1, keepdims=True)
        var = jnp.mean(jnp.square(h - mu), axis=-1, keepdims=True)
        return (h - mu) * jax.lax.rsqrt(var + 1e-05) * ln_g + ln_b

    def _L3_gnn_ref(x_feat, bases, W_pre, b_pre, W1, b1, W2, b2, src, dst):
        import jax, jax.numpy as jnp
        import numpy as np
        N_NODES = 50000
        N_EDGES = 25000
        HID = 96

        def _gelu(x):
            return jax.nn.gelu(x, approximate=False)
        n = x_feat.shape[0]
        h = _gelu(x_feat @ W_pre + b_pre)
        msg = h[src] * bases
        aggr = jax.ops.segment_sum(msg, dst, num_segments=n)
        x = x_feat + aggr
        y = _gelu(_gelu(x @ W1 + b1) @ W2 + b2)
        return x + y
    edge_index = jnp.stack([src, dst])
    h = jnp.maximum(_layernorm(x, axis=-1), 0.0)
    x = x + _L0_gnn_ref(h, edge_index, edge_weight, L0_gnn_W, L0_gnn_bias, L0_gnn_gamma, L0_gnn_beta)
    h = jnp.maximum(_layernorm(x, axis=-1), 0.0)
    x = x + _L1_gnn_ref(h, edge_index, L1_gnn_W0, L1_gnn_b0, L1_gnn_g0, L1_gnn_be0, L1_gnn_W1, L1_gnn_b1, L1_gnn_g1, L1_gnn_be1)
    h = jnp.maximum(_layernorm(x, axis=-1), 0.0)
    x = x + _L2_gnn_ref(h, edge_index, edge_attr_32, L2_gnn_mW1, L2_gnn_mb1, L2_gnn_mW2, L2_gnn_mb2, L2_gnn_gW1, L2_gnn_gb1, L2_gnn_gW2, L2_gnn_gb2, L2_gnn_uW1, L2_gnn_ub1, L2_gnn_uW2, L2_gnn_ub2, L2_gnn_ln_g, L2_gnn_ln_b)
    h = jnp.maximum(_layernorm(x, axis=-1), 0.0)
    x = x + _L3_gnn_ref(h, edge_attr_96, L3_gnn_W_pre, L3_gnn_b_pre, L3_gnn_W1, L3_gnn_b1, L3_gnn_W2, L3_gnn_b2, src, dst)
    return x

_drawn_inputs = setup_inputs


def setup_inputs(seed=0):
    import zlib

    import numpy as np

    out = dict(_drawn_inputs(seed))
    spreads = {'L0_gnn_bias': (0.0, 0.695),
     'L0_gnn_gamma': (1.0, 0.2),
     'L0_gnn_beta': (0.0, 0.1),
     'L1_gnn_b0': (0.0, 0.1),
     'L1_gnn_g0': (1.0, 0.2),
     'L1_gnn_be0': (0.0, 0.1),
     'L1_gnn_b1': (0.0, 0.1),
     'L1_gnn_g1': (1.0, 0.2),
     'L1_gnn_be1': (0.0, 0.1),
     'L2_gnn_mb1': (0.0, 0.1),
     'L2_gnn_mb2': (0.0, 0.1),
     'L2_gnn_gb1': (0.0, 2.0),
     'L2_gnn_ub1': (0.0, 0.472),
     'L2_gnn_ub2': (0.0, 0.1),
     'L2_gnn_ln_g': (1.0, 0.2),
     'L2_gnn_ln_b': (0.0, 0.1)}
    factors = {'edge_attr_32': 2.749,
     'L2_gnn_gW1': 7.006,
     'L2_gnn_gW2': 8.0,
     'L3_gnn_b_pre': 5.118,
     'L3_gnn_b1': 4.52,
     'L3_gnn_b2': 3.016}
    for name, (base, spread) in spreads.items():
        noise = np.random.default_rng([zlib.crc32(name.encode()), seed]).standard_normal(out[name].shape)
        drawn = base * np.exp(spread * noise) if base else spread * noise
        out[name] = jnp.asarray(drawn.astype(out[name].dtype))
    for name, factor in factors.items():
        out[name] = (out[name] * factor).astype(out[name].dtype)
    return out
```

```python
from contextlib import ExitStack, contextmanager

import concourse.bass as bass
from concourse import mybir

F32 = mybir.dt.float32
I32 = mybir.dt.int32
ALU = mybir.AluOpType
ACT = mybir.ActivationFunctionType
AX = mybir.AxisListType

P = 128
J = 8
GROUP = P * J
WIN = 64
BANK = 512
EPS = 1e-5
PER_BANK = 5
TURNS = 4
CHUNK = 500
SCATTER_BANK = 4


def node_split(n_nodes):
    parts = max(p for p in range(1, P + 1) if n_nodes % p == 0)
    return parts, n_nodes // parts


def group_count(n_edges):
    return 2 * -(-n_edges // (2 * GROUP))


def program(nc, D, out):
    N, F = D["x"].shape
    PN, C = node_split(N)
    G = D["src"].shape[0]
    PAIRS = G // 2
    F1 = F + 1
    ROUNDS = -(-N // WIN)
    assert C % PER_BANK == 0 and C <= 7 * TURNS and N + WIN <= 8 * BANK and F == 96
    BANKS = C // PER_BANK
    TBANKS = -(-C // TURNS)
    CHUNKS = [(k, min(CHUNK, N - k)) for k in range(0, N, CHUNK)]

    table = nc.dram_tensor("table", (N, F), F32, kind="Internal").ap()
    table2 = nc.dram_tensor("table2", (N, 2 * F), F32, kind="Internal").ap()

    ctx = ExitStack()
    with ctx:
        def sb(name, shape, dt=F32):
            return ctx.enter_context(nc.sbuf_tensor(name, shape, dt))

        x = sb("x", [PN, C, F])
        h = sb("h", [PN, C, F])
        t = sb("t", [PN, C, F])
        sq = sb("sq", [PN, C, F])
        pre = sb("pre", [PN, C, 2 * F])
        stat = sb("stat", [PN, C])
        var = sb("var", [PN, C])
        std = sb("std", [PN, C])
        rstd = sb("rstd", [PN, C])
        deg = sb("deg", [PN, C])
        dis = sb("dis", [PN, C])
        featT = sb("featT", [F1, N])
        aggT = sb("aggT", [F1, N + WIN])
        hidT = sb("hidT", [F1, N])
        dst_i = sb("dst_i", [P, G * J], I32)
        dst_f = sb("dst_f", [P, G * J])
        rel = sb("rel", [P, G * J])
        bad = sb("bad", [P, G * J])
        wgt = sb("wgt", [P, G * J])
        base_f = sb("base_f", [P, G])
        base_i = sb("base_i", [1, G], I32)
        base_r = sb("base_r", [1, G])
        bad_sum = sb("bad_sum", [P, 1])
        spread = sb("spread", [P, 1])
        fine = sb("fine", [P, 1])
        rounds_f = sb("rounds_f", [1, 1])
        rounds_i = sb("rounds_i", [1, 1], I32)
        idx = [sb(f"idx{b}", [P, J], I32) for b in range(2)]
        rows = [sb(f"rows{b}", [P, J, 2 * F]) for b in range(2)]
        msg = [sb(f"msg{b}", [P, J, F1]) for b in range(2)]
        gat = [sb(f"gat{b}", [P, J, F]) for b in range(2)]
        hot = [sb(f"hot{b}", [P, J, 2 * WIN]) for b in range(2)]
        attr = [sb(f"attr{b}", [P, J * F]) for b in range(2)]
        logit = [sb(f"logit{b}", [P, J]) for b in range(2)]
        tanh = [sb(f"tanh{b}", [P, J]) for b in range(2)]
        gate = [sb(f"gate{b}", [P, J]) for b in range(2)]
        ident = sb("ident", [P, P])
        ones = sb("ones", [P, P])
        iota = sb("iota", [P, WIN])
        iota_r = sb("iota_r", [P, WIN])

        def row_consts(name, width, parts=PN):
            return sb(name, [parts, width]), D[name].rearrange("(a f) -> a f", a=1).to_broadcast([parts, width])

        loads = []

        def vector_rows(name, parts=PN):
            tile_, src_ = row_consts(name, D[name].shape[0], parts)
            loads.append((tile_[:], src_))
            return tile_

        def vector_column(name):
            n = D[name].shape[0]
            tile_ = sb("col_" + name, [n, 1])
            loads.append((tile_[:], D[name].rearrange("(f a) -> f a", a=1)))
            return tile_

        def matrix(name, *parts):
            width = sum(D[w].shape[1] for w, _ in parts)
            with_bias = any(b for _, b in parts)
            tile_ = sb(name, [F1 if with_bias else F, width])
            at = 0
            for w, b in parts:
                n = D[w].shape[1]
                loads.append((tile_[0:F, at:at + n], D[w][0:F, :]))
                if b:
                    loads.append((tile_[F:F1, at:at + n], D[b].rearrange("(a f) -> a f", a=1)))
                at += n
            return tile_

        L0_bias, L0_gamma, L0_beta = (vector_rows("L0_gnn_" + k) for k in ("bias", "gamma", "beta"))
        L1_b = [vector_rows(f"L1_gnn_b{k}") for k in range(2)]
        L1_g = [vector_rows(f"L1_gnn_g{k}") for k in range(2)]
        L1_be = [vector_rows(f"L1_gnn_be{k}") for k in range(2)]
        L2_ub2, L2_g, L2_b = (vector_rows("L2_gnn_" + k) for k in ("ub2", "ln_g", "ln_b"))
        L2_ub1 = vector_column("L2_gnn_ub1")
        L3_b1 = vector_column("L3_gnn_b1")
        W0 = sb("W0", [F1, F1])
        loads.append((W0[0:F, 0:F], D["L0_gnn_W"]))
        W1 = [matrix(f"W1_{k}", (f"L1_gnn_W{k}", None)) for k in range(2)]
        W2in = matrix("W2in", ("L2_gnn_mW1", "L2_gnn_mb1"), ("L2_gnn_gW1", "L2_gnn_gb1"))
        W2msg = matrix("W2msg", ("L2_gnn_mW2", "L2_gnn_mb2"))
        W2u_x = sb("W2u_x", [F, F])
        W2u_a = sb("W2u_a", [F, F])
        loads.append((W2u_x[:], D["L2_gnn_uW1"][0:F, :]))
        loads.append((W2u_a[:], D["L2_gnn_uW1"][F:2 * F, :]))
        W2u2 = matrix("W2u2", ("L2_gnn_uW2", None))
        W3pre = matrix("W3pre", ("L3_gnn_W_pre", "L3_gnn_b_pre"))
        W3a = matrix("W3a", ("L3_gnn_W1", None))
        W3b = matrix("W3b", ("L3_gnn_W2", "L3_gnn_b2"))
        ED = D["L2_gnn_mW1"].shape[0] - F
        Q = P // ED
        assert ED == 32
        W2e = sb("W2e", [P, 2 * F])
        for q in range(Q):
            for k, w in enumerate(("L2_gnn_mW1", "L2_gnn_gW1")):
                loads.append((W2e[q * ED:(q + 1) * ED, k * F:(k + 1) * F], D[w][F:F + ED, :]))
        gW2 = sb("gW2", [P, F])
        loads.append((gW2[:], D["L2_gnn_gW2"].rearrange("f a -> a f").to_broadcast([P, F])))
        gb2 = sb("gb2", [P, 1])
        half_gb2 = sb("half_gb2", [P, 1])
        loads.append((gb2[:], D["L2_gnn_gb2"].rearrange("(a f) -> a f", a=1).to_broadcast([P, 1])))

        ps = ctx.enter_context(nc.psum_tensor("ps", [P, 8, BANK], F32))

        def by_tile(T, rows_):
            return T[0:rows_, 0:N].rearrange("f (p c) -> f c p", c=C)

        def banks(width):
            return ps[0:PN, 0:BANKS, 0:PER_BANK * width].rearrange("p b (k m) -> p b k m", m=width)

        def in_banks(T):
            return T.rearrange("p (b k) m -> p b k m", k=PER_BANK)

        def bank_rows(T):
            return T[:].unsqueeze(1).unsqueeze(1).to_broadcast([PN, BANKS, PER_BANK, F])

        def node_rows(T):
            return T[:].unsqueeze(1).to_broadcast([PN, C, F])

        def per_node(T, width=F):
            return T[:].unsqueeze(2).to_broadcast([PN, C, width])

        @contextmanager
        def signals(*names):
            with ExitStack() as s:
                sems = [s.enter_context(nc.semaphore(n)) for n in names]
                yield sems
                for one in sems:
                    nc.sync.sem_clear(one)
                nc.all_engine_barrier(sem_only=True)

        def linker(engine, sem):
            count = [0]

            def link(ins):
                count[0] += 1
                ins.then_inc(sem, 1)
                engine.wait_ge(sem, count[0])
            return link

        def center_scale(dve, link, src, dst, var_ready, std_ready, k):
            link(nc.vector.tensor_reduce(stat[:], src[:], AX.X, ALU.add))
            link(nc.vector.tensor_scalar(stat[:], stat[:], -1.0 / F, None, ALU.mult))
            link(nc.vector.tensor_tensor(dst[:], src[:], per_node(stat), ALU.add))
            link(nc.vector.tensor_tensor(sq[:], dst[:], dst[:], ALU.mult))
            link(nc.vector.tensor_reduce(var[:], sq[:], AX.X, ALU.add))
            nc.vector.tensor_scalar(var[:], var[:], 1.0 / F, EPS, ALU.mult, ALU.add).then_inc(var_ready, 1)
            dve.wait_ge(std_ready, k + 1)
            link(nc.vector.reciprocal(rstd[:], std[:]))
            link(nc.vector.tensor_tensor(dst[:], dst[:], per_node(rstd), ALU.mult))

        def root(act, var_ready, std_ready, k):
            act.wait_ge(var_ready, k + 1)
            nc.scalar.activation(std[:], var[:], ACT.Sqrt).then_inc(std_ready, 1)

        def project(pe, T, rows_, W, width, done):
            tiles = by_tile(T, rows_)
            for c in range(C):
                at = (c % PER_BANK) * width
                mm = pe.matmul(ps[0:PN, c // PER_BANK, at:at + width], tiles[:, c, :], W[0:rows_, 0:width],
                               start=True, stop=True)
            mm.then_inc(done, 1)

        def turn(pe, T, done):
            for c in range(C):
                at = (c % TURNS) * PN
                mm = pe.transpose(ps[0:F, c // TURNS, at:at + PN], T[:, c, :], ident[0:PN, 0:PN])
                if c % TURNS == TURNS - 1 or c == C - 1:
                    mm.then_inc(done, 1)

        def turned(k):
            n = min(TURNS, C - TURNS * k)
            return ps[0:F, k, 0:n * PN].rearrange("f (k p) -> f k p", p=PN)

        def turned_home(T, k):
            return by_tile(T, F)[:, TURNS * k:min(C, TURNS * (k + 1)), :]

        def first_window():
            nc.vector.tensor_copy(iota_r[:], iota[:])
            nc.vector.tensor_copy(base_r[:], base_f[0:1, :])
            nc.vector.tensor_copy(base_i[:], base_f[0:1, :])

        with signals("s_x", "s_dst", "s_loads", "s_zero", "s_const", "s_steps", "s_var", "s_std", "s_h", "s_w0",
                     "s_dstf", "s_base", "s_rel", "s_bad", "s_spread", "s_fine", "s_hgb") as S:
            (x_in, dst_in, loaded, zeroed, consts, steps, var_ready, std_ready, h_ready, w0_zero,
             dstf_ready, base_ready, rel_done, bad_ready, spread_ready, stored, hgb) = S
            with nc.Block() as block:
                @block.sync
                def _(sp):
                    sp.dma_start(x[:], D["x"].rearrange("(p c) f -> p c f", c=C)).then_inc(x_in, 16)
                    sp.dma_start(dst_i[:], D["dst"]).then_inc(dst_in, 16)
                    sp.dma_start(wgt[:], D["edge_weight"]).then_inc(loaded, 16)
                    sp.wait_ge(w0_zero, 1)
                    for to, fro in loads:
                        with nc.allow_non_contiguous_dma(reason="columns of biases"):
                            sp.dma_start(to, fro).then_inc(loaded, 16)
                    sp.wait_ge(h_ready, 1)
                    sp.dma_start(table.rearrange("(p c) f -> p c f", c=C), h[:]).then_inc(stored, 16)
                    sp.wait_ge(stored, 16)
                    sp.wait_ge(loaded, 16 * (len(loads) + 1))

                @block.gpsimd
                def _(pool):
                    link = linker(pool, zeroed)
                    link(nc.gpsimd.memset(W0[:], 0.0))
                    nc.gpsimd.memset(W0[F:F1, F:F1], 1.0).then_inc(w0_zero, 1)
                    pool.wait_ge(w0_zero, 1)
                    link(nc.gpsimd.memset(ident[:], 0.0))
                    link(nc.gpsimd.affine_select(out=ident[:], in_=ident[:], compare_op=ALU.not_equal, fill=1.0,
                                                 base=0, pattern=[[-1, P]], channel_multiplier=1))
                    link(nc.gpsimd.memset(ones[:], 1.0))
                    nc.gpsimd.iota(iota[:], [[1, WIN]], base=0, channel_multiplier=0,
                                   allow_small_or_imprecise_dtypes=True).then_inc(consts, 1)
                    pool.wait_ge(consts, 1)
                    link(nc.gpsimd.memset(featT[F:F1, :], 1.0))
                    link(nc.gpsimd.memset(hidT[F:F1, :], 1.0))
                    link(nc.gpsimd.memset(aggT[:], 0.0))
                    for b in range(2):
                        link(nc.gpsimd.memset(msg[b][:, :, F:F1], 1.0))
                        link(nc.gpsimd.memset(rows[b][:, :, F:F1], 1.0))

                @block.tensor
                def _(pe):
                    pe.wait_ge(consts, 1)
                    pe.wait_ge(dstf_ready, 1)
                    pe.matmul(ps[:, 0, 0:G], ones[0:1, :],
                              dst_f[0:1, :].rearrange("p (g j) -> p g j", j=J)[:, :, 0],
                              start=True, stop=True).then_inc(base_ready, 1)
                    pe.wait_ge(bad_ready, 1)
                    pe.matmul(ps[:, 1, 0:1], ones[:], bad_sum[:], start=True, stop=True).then_inc(spread_ready, 1)

                @block.scalar
                def _(act):
                    root(act, var_ready, std_ready, 0)

                @block.vector
                def _(dve):
                    link = linker(dve, steps)
                    dve.wait_ge(x_in, 16)
                    center_scale(dve, link, x, h, var_ready, std_ready, 0)
                    nc.vector.tensor_scalar(h[:], h[:], 0.0, None, ALU.max).then_inc(h_ready, 1)
                    dve.wait_ge(dst_in, 16)
                    nc.vector.tensor_copy(dst_f[:], dst_i[:]).then_inc(dstf_ready, 1)
                    dve.wait_ge(base_ready, 1)
                    dve.wait_ge(dstf_ready, 1)
                    link(nc.vector.tensor_copy(base_f[:], ps[:, 0, 0:G]))
                    grouped = rel[:].rearrange("p (g j) -> p g j", j=J)
                    link(nc.vector.tensor_tensor(grouped, dst_f[:].rearrange("p (g j) -> p g j", j=J),
                                                 base_f[:].unsqueeze(2).to_broadcast([P, G, J]), ALU.subtract))
                    link(nc.vector.tensor_scalar(bad[:], rel[:], 0.0, None, ALU.is_lt))
                    link(nc.vector.scalar_tensor_tensor(out=bad[:], in0=rel[:], scalar=float(WIN), in1=bad[:],
                                                        op0=ALU.is_ge, op1=ALU.max))
                    link(nc.vector.scalar_tensor_tensor(out=bad[:], in0=dst_f[:], scalar=0.0, in1=bad[:],
                                                        op0=ALU.is_ge, op1=ALU.mult))
                    nc.vector.tensor_reduce(bad_sum[:], bad[:], AX.X, ALU.add).then_inc(bad_ready, 1)
                    dve.wait_ge(spread_ready, 1)
                    link(nc.vector.tensor_scalar(fine[:], ps[:, 1, 0:1], 0.5, None, ALU.is_lt))
                    link(nc.vector.tensor_scalar(rounds_f[:], fine[0:1, :], float(1 - ROUNDS), float(ROUNDS),
                                                 ALU.mult, ALU.add))
                    nc.vector.tensor_copy(rounds_i[:], rounds_f[:])
                    link(nc.vector.tensor_scalar(base_f[:], base_f[:], fine[:, 0:1], None, ALU.mult))
                    nc.vector.tensor_tensor(grouped, dst_f[:].rearrange("p (g j) -> p g j", j=J),
                                            base_f[:].unsqueeze(2).to_broadcast([P, G, J]), ALU.subtract)
                    dve.wait_ge(consts, 1)
                    first_window()
                    dve.wait_ge(loaded, 16 * (len(loads) + 1))
                    nc.vector.tensor_scalar(half_gb2[:], gb2[:], 0.5, None, ALU.mult)

        rounds = nc.values_load(rounds_i[0:1, 0:1], min_val=1, max_val=ROUNDS)

        def edge_pass(layer):
            wide = layer == "L2"
            source = table2 if wide else table
            width = 2 * F if wide else F
            out_rows = F1 if layer in ("L0", "L2") else F
            adds = 2 if layer == "L0" else 1
            takes = {"L0": rows, "L1": rows, "L2": msg, "L3": msg}[layer]
            names = ["idx_in", "attr_in", "gathered", "hot_raw", "hot_ready", "scattered", "added", "rows_used",
                     "mlp_ready", "gate_act", "msg_act", "weighed", "logit_ready", "tanh_ready", "gate_ready",
                     "slot_open"]
            with nc.Fori(0, rounds), signals(*[f"s_{n}{b}" for n in names for b in range(2)], "s_moved") as S:
                moved = S[-1]
                (idx_in, attr_in, gathered, hot_raw, hot_ready, scattered, added, rows_used, mlp_ready,
                 gate_act, msg_act, weighed, logit_ready, tanh_ready, gate_ready, slot_open) = (S[2 * k:2 * k + 2]
                                                                                     for k in range(len(names)))

                def free(i):
                    return i + 1

                def done(i):
                    return i + 2

                with nc.Block() as block:
                    @block.sync
                    def _(sp):
                        with sp.Fori(0, PAIRS) as i:
                            for b in range(2):
                                sp.wait_ge((scattered if layer in ("L0", "L1") else rows_used)[b], free(i))
                                sp.dma_start(idx[b][:], D["src"][bass.ds(2 * i + b, 1)].rearrange(
                                    "a p j -> (a p) j")).then_inc(idx_in[b], 16)
                                if layer == "L2":
                                    sp.wait_ge(mlp_ready[b], free(i))
                                    sp.dma_start(attr[b][:, 0:GROUP * ED // P], D["edge_attr_32"][
                                        bass.ds(2 * i + b, 1)].rearrange("a p m -> (a p) m")).then_inc(attr_in[b], 16)
                                if layer == "L3":
                                    sp.wait_ge(rows_used[b], free(i))
                                    sp.dma_start(attr[b][:], D["edge_attr_96"][
                                        bass.ds(2 * i + b, 1)].rearrange("a p m -> (a p) m")).then_inc(attr_in[b], 16)

                    @block.gpsimd
                    def _(pool):
                        with pool.Fori(0, PAIRS) as i:
                            for b in range(2):
                                pool.wait_ge(idx_in[b], 16 * (i + 1))
                                if layer in ("L0", "L1"):
                                    pool.wait_ge(scattered[b], free(i))
                                elif layer == "L2":
                                    pool.wait_ge(msg_act[b], free(i))
                                    pool.wait_ge(gate_act[b], free(i))
                                else:
                                    pool.wait_ge(rows_used[b], free(i))
                                pool.sem_inc(slot_open[b], 1)
                                for j in range(J):
                                    pool.indirect_dma_start(
                                        rows[b][:, j, 0:width], None, source,
                                        bass.IndirectOffsetOnAxis(ap=idx[b][:, j:j + 1], axis=0),
                                    ).then_inc(gathered[b], 16)
                        for b in range(2):
                            pool.wait_ge(gathered[b], 16 * J * PAIRS)
                        for b in range(2):
                            pool.dma_reset(range(gathered[b].num, gathered[b].num + 1))

                    @block.tensor
                    def _(pe):
                        def edge_products(i, b):
                            pe.wait_ge(attr_in[b], 16 * (i + 1))
                            pe.wait_ge(rows_used[1 - b], free(i) if b == 0 else done(i))
                            for k in range(J // Q):
                                for q in range(Q):
                                    mm = pe.matmul(ps[:, q, k * 2 * F:(k + 1) * 2 * F],
                                                   attr[b][q * ED:(q + 1) * ED, k * P:(k + 1) * P],
                                                   W2e[q * ED:(q + 1) * ED, :], start=True, stop=True,
                                                   tile_position=(q * ED, 0))
                            mm.then_inc(mlp_ready[b], 1)

                        def scatter(i, b):
                            if layer in ("L0", "L1"):
                                pe.wait_ge(gathered[b], 16 * J * (i + 1))
                            elif layer == "L2":
                                pe.wait_ge(msg_act[b], done(i))
                            else:
                                pe.wait_ge(rows_used[b], done(i))
                            pe.wait_ge(hot_ready[b], i + 1)
                            pe.wait_ge(added[b], adds * i + 1)
                            cols = 2 * WIN if layer == "L0" else WIN
                            for j in range(J):
                                mm = pe.matmul(ps[0:out_rows, SCATTER_BANK + b, 0:cols], takes[b][:, j, 0:out_rows],
                                               hot[b][:, j, 0:cols], start=(j == 0), stop=(j == J - 1))
                            mm.then_inc(scattered[b], 1)

                        for b in range(2):
                            pe.sem_inc(scattered[b], 1)
                            pe.sem_inc(mlp_ready[b], 1)
                        if layer == "L2":
                            edge_products(0, 0)
                            with pe.Fori(0, PAIRS - 1) as i:
                                edge_products(i, 1)
                                scatter(i, 0)
                                edge_products(i + 1, 0)
                                scatter(i, 1)
                            edge_products(PAIRS - 1, 1)
                            scatter(PAIRS - 1, 0)
                            scatter(PAIRS - 1, 1)
                        else:
                            with pe.Fori(0, PAIRS) as i:
                                for b in range(2):
                                    scatter(i, b)

                    if layer == "L2":
                        @block.scalar
                        def _(act):
                            for b in range(2):
                                act.sem_inc(gate_act[b], 1)
                                act.sem_inc(msg_act[b], 1)
                            with act.Fori(0, PAIRS) as i:
                                for b in range(2):
                                    act.wait_ge(rows_used[b], done(i))
                                    act.wait_ge(logit_ready[b], free(i))
                                    nc.scalar.activation(gat[b][:], rows[b][:, :, F:2 * F],
                                                         ACT.Gelu).then_inc(gate_act[b], 1)
                                    act.wait_ge(scattered[b], free(i))
                                    nc.scalar.activation(msg[b][:, :, 0:F], rows[b][:, :, 0:F],
                                                         ACT.Gelu).then_inc(msg_act[b], 1)
                                    act.wait_ge(logit_ready[b], done(i))
                                    nc.scalar.activation(tanh[b][:], logit[b][:], ACT.Tanh, bias=half_gb2[:, 0:1],
                                                         scale=0.5).then_inc(tanh_ready[b], 1)

                    @block.vector
                    def _(dve):
                        for b in range(2):
                            dve.sem_inc(rows_used[b], 1)
                            dve.sem_inc(logit_ready[b], 1)
                            dve.sem_inc(added[b], 1)
                        with dve.Fori(0, PAIRS) as i:
                            for b in range(2):
                                g = 2 * i + b
                                first = dve.value_load(base_i[0:1, bass.ds(g, 1)], min_val=0, max_val=N)
                                raw = hot[b][:, :, WIN:2 * WIN] if layer in ("L0", "L2") else hot[b][:, :, 0:WIN]
                                dve.wait_ge(scattered[b], free(i))
                                made = nc.vector.tensor_tensor(
                                    raw, rel[:, bass.ds(g * J, J)].unsqueeze(2).to_broadcast([P, J, WIN]),
                                    iota_r[:].unsqueeze(1).to_broadcast([P, J, WIN]), ALU.is_equal)
                                if layer in ("L1", "L3"):
                                    made.then_inc(hot_ready[b], 1)
                                else:
                                    made.then_inc(hot_raw[b], 1)
                                if layer == "L0":
                                    dve.wait_ge(hot_raw[b], i + 1)
                                    nc.vector.tensor_tensor(
                                        hot[b][:, :, 0:WIN], raw,
                                        wgt[:, bass.ds(g * J, J)].unsqueeze(2).to_broadcast([P, J, WIN]),
                                        ALU.mult).then_inc(hot_ready[b], 1)
                                if layer == "L3":
                                    dve.wait_ge(gathered[b], 16 * J * (i + 1))
                                    dve.wait_ge(attr_in[b], 16 * (i + 1))
                                    nc.vector.tensor_tensor(
                                        msg[b][:, :, 0:F], rows[b][:, :, 0:F],
                                        attr[b][:].rearrange("p (j f) -> p j f", f=F), ALU.mult,
                                    ).then_inc(rows_used[b], 1)
                                if layer == "L2":
                                    dve.wait_ge(gathered[b], 16 * J * (i + 1))
                                    dve.wait_ge(mlp_ready[b], done(i))
                                    sums = rows[b][:].rearrange("p (k q) f -> p q k f", q=Q)
                                    prods = ps[:, 0:Q, 0:J // Q * 2 * F].rearrange("p q (k f) -> p q k f", f=2 * F)
                                    nc.vector.tensor_tensor(sums, prods, sums, ALU.add).then_inc(rows_used[b], 1)
                                    dve.wait_ge(gate_act[b], done(i))
                                    nc.vector.tensor_tensor(gat[b][:], gat[b][:],
                                                            gW2[:].unsqueeze(1).to_broadcast([P, J, F]),
                                                            ALU.mult).then_inc(weighed[b], 1)
                                    dve.wait_ge(weighed[b], i + 1)
                                    nc.vector.tensor_reduce(logit[b][:], gat[b][:], AX.X,
                                                            ALU.add).then_inc(logit_ready[b], 1)
                                    dve.wait_ge(tanh_ready[b], i + 1)
                                    nc.vector.tensor_scalar(gate[b][:], tanh[b][:], 0.5, 0.5, ALU.mult,
                                                            ALU.add).then_inc(gate_ready[b], 1)
                                    dve.wait_ge(gate_ready[b], i + 1)
                                    dve.wait_ge(hot_raw[b], i + 1)
                                    nc.vector.tensor_tensor(hot[b][:, :, 0:WIN], raw,
                                                            gate[b][:].unsqueeze(2).to_broadcast([P, J, WIN]),
                                                            ALU.mult).then_inc(hot_ready[b], 1)
                                dve.wait_ge(scattered[b], done(i))
                                dve.wait_ge(added[1 - b], adds * i + 1 if b == 0 else adds * (i + 1) + 1)
                                wide_rows = F if layer == "L0" else out_rows
                                home = aggT[0:wide_rows, bass.ds(first, WIN)]
                                nc.vector.tensor_tensor(home, ps[0:wide_rows, SCATTER_BANK + b, 0:WIN], home,
                                                        ALU.add).then_inc(added[b], 1)
                                if layer == "L0":
                                    home = aggT[F:F1, bass.ds(first, WIN)]
                                    nc.vector.tensor_tensor(home, ps[F:F1, SCATTER_BANK + b, WIN:2 * WIN], home,
                                                            ALU.add).then_inc(added[b], 1)
                        nc.vector.tensor_scalar(iota_r[:], iota_r[:], float(WIN), None, ALU.add)
                        nc.vector.tensor_scalar(base_r[:], base_r[:], float(WIN), None,
                                                ALU.add).then_inc(moved, 1)
                        dve.wait_ge(moved, 1)
                        nc.vector.tensor_copy(base_i[:], base_r[:])

        def finish_layer_norm(dve, link, gamma, beta):
            link(nc.vector.tensor_tensor(t[:], t[:], node_rows(gamma), ALU.mult))
            link(nc.vector.tensor_tensor(t[:], t[:], node_rows(beta), ALU.add))

        edge_pass("L0")

        with signals("s_proj", "s_steps", "s_var", "s_std", "s_h", "s_turned", "s_deg", "s_sdeg", "s_stored") as S:
            projected, steps, var_ready, std_ready, h_ready, turn_done, deg_ready, sdeg, stored = S
            with nc.Block() as block:
                @block.tensor
                def _(pe):
                    project(pe, aggT, F1, W0, F1, projected)
                    pe.wait_ge(h_ready, 1)
                    turn(pe, h, turn_done)

                @block.scalar
                def _(act):
                    act.wait_ge(deg_ready, 1)
                    nc.scalar.activation(std[:], deg[:], ACT.Sqrt).then_inc(sdeg, 1)
                    root(act, var_ready, std_ready, 0)
                    root(act, var_ready, std_ready, 1)

                @block.vector
                def _(dve):
                    link = linker(dve, steps)
                    dve.wait_ge(projected, 1)
                    nc.vector.tensor_scalar(deg[:].rearrange("p (b k) -> p b k", k=PER_BANK), banks(F1)[:, :, :, F],
                                            1.0, None, ALU.add).then_inc(deg_ready, 1)
                    dve.wait_ge(sdeg, 1)
                    link(nc.vector.reciprocal(dis[:], std[:]))
                    link(nc.vector.tensor_tensor(in_banks(t[:]), banks(F1)[:, :, :, 0:F], bank_rows(L0_bias), ALU.add))
                    center_scale(dve, link, t, t, var_ready, std_ready, 0)
                    finish_layer_norm(dve, link, L0_gamma, L0_beta)
                    link(nc.vector.tensor_tensor(x[:], x[:], t[:], ALU.add))
                    center_scale(dve, link, x, h, var_ready, std_ready, 1)
                    link(nc.vector.tensor_scalar(h[:], h[:], 0.0, None, ALU.max))
                    nc.vector.tensor_tensor(h[:], h[:], per_node(dis), ALU.mult).then_inc(h_ready, 1)
                    for k in range(TBANKS):
                        dve.wait_ge(turn_done, k + 1)
                        nc.vector.tensor_copy(turned_home(aggT, k), turned(k))
                    first_window()

                @block.sync
                def _(sp):
                    sp.wait_ge(h_ready, 1)
                    sp.dma_start(table.rearrange("(p c) f -> p c f", c=C), h[:]).then_inc(stored, 16)
                    sp.wait_ge(stored, 16)

        edge_pass("L1")

        def l1_tail(dve, link, k, projected, var_ready, std_ready, z_ready, tanh_done):
            dve.wait_ge(projected, 1)
            nc_dis = dis[:].rearrange("p (b k) -> p b k", k=PER_BANK).unsqueeze(3).to_broadcast(
                [PN, BANKS, PER_BANK, F])
            link(nc.vector.tensor_tensor(in_banks(t[:]), banks(F), nc_dis, ALU.mult))
            nc.vector.tensor_tensor(t[:], t[:], node_rows(L1_b[k]), ALU.add).then_inc(z_ready, 1)
            dve.wait_ge(tanh_done, 1)
            center_scale(dve, link, h, t, var_ready, std_ready, 0)
            finish_layer_norm(dve, link, L1_g[k], L1_be[k])

        with signals("s_proj", "s_steps", "s_var", "s_std", "s_h", "s_turned", "s_z", "s_tanh", "s_stored") as S:
            projected, steps, var_ready, std_ready, h_ready, turn_done, z_ready, tanh_done, stored = S
            with nc.Block() as block:
                @block.tensor
                def _(pe):
                    project(pe, aggT, F, W1[0], F, projected)
                    pe.wait_ge(h_ready, 1)
                    turn(pe, h, turn_done)

                @block.scalar
                def _(act):
                    act.wait_ge(z_ready, 1)
                    nc.scalar.activation(h[:], t[:], ACT.Tanh).then_inc(tanh_done, 1)
                    root(act, var_ready, std_ready, 0)

                @block.vector
                def _(dve):
                    link = linker(dve, steps)
                    l1_tail(dve, link, 0, projected, var_ready, std_ready, z_ready, tanh_done)
                    nc.vector.tensor_tensor(h[:], t[:], per_node(dis), ALU.mult).then_inc(h_ready, 1)
                    for k in range(TBANKS):
                        dve.wait_ge(turn_done, k + 1)
                        nc.vector.tensor_copy(turned_home(aggT, k), turned(k))
                    first_window()

                @block.sync
                def _(sp):
                    sp.wait_ge(h_ready, 1)
                    sp.dma_start(table.rearrange("(p c) f -> p c f", c=C), h[:]).then_inc(stored, 16)
                    sp.wait_ge(stored, 16)

        edge_pass("L1")

        PRE_TILES = 8
        PRE_STEPS = [(k, min(PRE_TILES, C - k)) for k in range(0, C, PRE_TILES)]
        with signals("s_proj", "s_steps", "s_var", "s_std", "s_h", "s_turned", "s_z", "s_tanh", "s_feat", "s_pre",
                     "s_pret", "s_stored") as S:
            (projected, steps, var_ready, std_ready, h_ready, turn_done, z_ready, tanh_done, feat_ready, pre_done,
             pre_taken, stored) = S
            with nc.Block() as block:
                @block.tensor
                def _(pe):
                    project(pe, aggT, F, W1[1], F, projected)
                    pe.wait_ge(h_ready, 1)
                    turn(pe, h, turn_done)
                    pe.wait_ge(feat_ready, TBANKS)
                    tiles = by_tile(featT, F1)
                    for s, (c0, n) in enumerate(PRE_STEPS):
                        if s >= 2:
                            pe.wait_ge(pre_taken, s - 1)
                        for c in range(c0, c0 + n):
                            k = c - c0
                            mm = pe.matmul(ps[0:PN, 4 * (s % 2) + k // 2, (k % 2) * 2 * F:(k % 2 + 1) * 2 * F],
                                           tiles[:, c, :], W2in[:], start=True, stop=True)
                        mm.then_inc(pre_done, 1)

                @block.scalar
                def _(act):
                    act.wait_ge(z_ready, 1)
                    nc.scalar.activation(h[:], t[:], ACT.Tanh).then_inc(tanh_done, 1)
                    root(act, var_ready, std_ready, 0)
                    root(act, var_ready, std_ready, 1)

                @block.vector
                def _(dve):
                    link = linker(dve, steps)
                    l1_tail(dve, link, 1, projected, var_ready, std_ready, z_ready, tanh_done)
                    link(nc.vector.tensor_tensor(x[:], x[:], t[:], ALU.add))
                    center_scale(dve, link, x, h, var_ready, std_ready, 1)
                    nc.vector.tensor_scalar(h[:], h[:], 0.0, None, ALU.max).then_inc(h_ready, 1)
                    for k in range(TBANKS):
                        dve.wait_ge(turn_done, k + 1)
                        nc.vector.tensor_copy(turned_home(featT, k), turned(k)).then_inc(feat_ready, 1)
                    first_window()
                    nc.vector.memset(aggT[:], 0.0)
                    for s, (c0, n) in enumerate(PRE_STEPS):
                        dve.wait_ge(pre_done, s + 1)
                        for k in range(0, n, 2):
                            m = min(2, n - k)
                            last = nc.vector.tensor_copy(
                                pre[:, c0 + k:c0 + k + m, :],
                                ps[0:PN, 4 * (s % 2) + k // 2, 0:m * 2 * F].rearrange("p (k f) -> p k f", k=m))
                        last.then_inc(pre_taken, 1)

                @block.sync
                def _(sp):
                    sp.wait_ge(pre_taken, len(PRE_STEPS))
                    sp.dma_start(table2.rearrange("(p c) f -> p c f", c=C), pre[:]).then_inc(stored, 16)
                    sp.wait_ge(stored, 16)

        edge_pass("L2")

        with signals("s_agg", "s_aggt", "s_hid", "s_hidt", "s_proj", "s_steps", "s_var", "s_std", "s_h", "s_turned",
                     "s_feat", "s_pre", "s_tab", "s_stored") as S:
            (agg_done, agg_taken, hid_done, hid_taken, projected, steps, var_ready, std_ready, h_ready, turn_done,
             feat_ready, pre_done, table_ready, stored) = S
            with nc.Block() as block:
                @block.tensor
                def _(pe):
                    for n, (at, w) in enumerate(CHUNKS):
                        pe.matmul(ps[0:F, n, 0:w], W2msg[:], aggT[0:F1, at:at + w], start=True,
                                  stop=True).then_inc(agg_done, 1)
                    for n, (at, w) in enumerate(CHUNKS):
                        pe.wait_ge(agg_taken, n + 1)
                        pe.matmul(ps[0:F, n, 0:w], W2u_x[:], featT[0:F, at:at + w], start=True, stop=False)
                        pe.matmul(ps[0:F, n, 0:w], W2u_a[:], aggT[0:F, at:at + w], start=False,
                                  stop=True).then_inc(hid_done, 1)
                    pe.wait_ge(hid_taken, len(CHUNKS))
                    project(pe, hidT, F, W2u2, F, projected)
                    pe.wait_ge(h_ready, 1)
                    turn(pe, h, turn_done)
                    pe.wait_ge(feat_ready, TBANKS)
                    project(pe, featT, F1, W3pre, F, pre_done)

                @block.scalar
                def _(act):
                    for n, (at, w) in enumerate(CHUNKS):
                        act.wait_ge(hid_done, n + 1)
                        nc.scalar.activation(hidT[0:F, at:at + w], ps[0:F, n, 0:w], ACT.Gelu,
                                             bias=L2_ub1[:, 0:1]).then_inc(hid_taken, 1)
                    root(act, var_ready, std_ready, 0)
                    root(act, var_ready, std_ready, 1)
                    act.wait_ge(pre_done, 1)
                    nc.scalar.activation(in_banks(t[:]), banks(F), ACT.Gelu).then_inc(table_ready, 1)

                @block.vector
                def _(dve):
                    link = linker(dve, steps)
                    for n, (at, w) in enumerate(CHUNKS):
                        dve.wait_ge(agg_done, n + 1)
                        nc.vector.tensor_copy(aggT[0:F, at:at + w], ps[0:F, n, 0:w]).then_inc(agg_taken, 1)
                    dve.wait_ge(projected, 1)
                    link(nc.vector.tensor_tensor(in_banks(t[:]), banks(F), bank_rows(L2_ub2), ALU.add))
                    link(nc.vector.tensor_tensor(t[:], t[:], h[:], ALU.add))
                    center_scale(dve, link, t, t, var_ready, std_ready, 0)
                    finish_layer_norm(dve, link, L2_g, L2_b)
                    link(nc.vector.tensor_tensor(x[:], x[:], t[:], ALU.add))
                    center_scale(dve, link, x, h, var_ready, std_ready, 1)
                    nc.vector.tensor_scalar(h[:], h[:], 0.0, None, ALU.max).then_inc(h_ready, 1)
                    for k in range(TBANKS):
                        dve.wait_ge(turn_done, k + 1)
                        nc.vector.tensor_copy(turned_home(featT, k), turned(k)).then_inc(feat_ready, 1)
                    first_window()
                    nc.vector.memset(aggT[:], 0.0)

                @block.sync
                def _(sp):
                    sp.wait_ge(table_ready, 1)
                    sp.dma_start(table.rearrange("(p c) f -> p c f", c=C), t[:]).then_inc(stored, 16)
                    sp.wait_ge(stored, 16)

        edge_pass("L3")

        with signals("s_sum", "s_hid", "s_hidt", "s_proj", "s_xt", "s_y", "s_xd", "s_steps", "s_out", "s_stored") as S:
            sum_ready, hid_done, hid_taken, projected, x_turned, y_ready, x_taken, steps, out_ready, stored = S
            with nc.Block() as block:
                @block.tensor
                def _(pe):
                    for n, (at, w) in enumerate(CHUNKS):
                        pe.wait_ge(sum_ready, n + 1)
                        pe.matmul(ps[0:F, n, 0:w], W3a[:], aggT[0:F, at:at + w], start=True,
                                  stop=True).then_inc(hid_done, 1)
                    pe.wait_ge(hid_taken, len(CHUNKS))
                    project(pe, hidT, F1, W3b, F, projected)
                    pe.wait_ge(y_ready, 1)
                    project(pe, aggT, F, ident, F, x_turned)

                @block.scalar
                def _(act):
                    for n, (at, w) in enumerate(CHUNKS):
                        act.wait_ge(hid_done, n + 1)
                        nc.scalar.activation(hidT[0:F, at:at + w], ps[0:F, n, 0:w], ACT.Gelu,
                                             bias=L3_b1[:, 0:1]).then_inc(hid_taken, 1)
                    act.wait_ge(projected, 1)
                    nc.scalar.activation(in_banks(t[:]), banks(F), ACT.Gelu).then_inc(y_ready, 1)

                @block.vector
                def _(dve):
                    link = linker(dve, steps)
                    for n, (at, w) in enumerate(CHUNKS):
                        nc.vector.tensor_tensor(aggT[0:F, at:at + w], featT[0:F, at:at + w], aggT[0:F, at:at + w],
                                                ALU.add).then_inc(sum_ready, 1)
                    dve.wait_ge(y_ready, 1)
                    link(nc.vector.tensor_tensor(x[:], x[:], t[:], ALU.add))
                    dve.wait_ge(x_turned, 1)
                    nc.vector.tensor_tensor(in_banks(x[:]), banks(F), in_banks(x[:]), ALU.add).then_inc(out_ready, 1)

                @block.sync
                def _(sp):
                    sp.wait_ge(out_ready, 1)
                    sp.dma_start(out.rearrange("(p c) f -> p c f", c=C), x[:]).then_inc(stored, 16)
                    sp.wait_ge(stored, 16)


def kernel(**inputs):
    import numpy as _np
    import concourse.bacc as _bacc
    from concourse import mybir as _mybir
    from concourse.bass_utils import run_bass_kernel_spmd as _run

    arrays = {k: _np.asarray(v) for k, v in inputs.items()}
    n_edges = arrays["src"].shape[0]
    groups = group_count(n_edges)

    def padded(a, fill):
        full = _np.full((groups * GROUP,) + a.shape[1:], fill, a.dtype)
        full[:n_edges] = a
        return full

    arrays["src"] = padded(arrays["src"], 0).reshape(groups, P, J)
    for name, fill in (("dst", -1), ("edge_weight", 0)):
        arrays[name] = padded(arrays[name], fill).reshape(groups, P, J).transpose(1, 0, 2).reshape(P, groups * J)
    arrays["edge_attr_96"] = padded(arrays["edge_attr_96"], 0).reshape(groups, P, -1)
    a = padded(arrays["edge_attr_32"], 0)
    f = a.shape[1]
    q = P // f
    arrays["edge_attr_32"] = a.reshape(groups, P, J // q, q, f).transpose(0, 3, 4, 2, 1).reshape(groups, P, -1)

    nc = _bacc.Bacc("TRN2", target_bir_lowering=False, num_devices=1)
    feeds, D = {}, {}
    for name, a in arrays.items():
        a = _np.ascontiguousarray(a)
        feeds[f"in_{name}"] = a
        D[name] = nc.dram_tensor(f"in_{name}", a.shape, _mybir.dt.from_np(a.dtype), kind="ExternalInput").ap()
    out = nc.dram_tensor("out_x", inputs["x"].shape, F32, kind="ExternalOutput").ap()
    program(nc, D, out)
    r = _run(nc, [feeds], core_ids=[0])
    return r.results[0]["out_x"]
```

```python
from contextlib import ExitStack, contextmanager

import concourse.bass as bass
from concourse import mybir

F32 = mybir.dt.float32
F16 = mybir.dt.float16
BF16 = mybir.dt.bfloat16
I32 = mybir.dt.int32
ALU = mybir.AluOpType
ACT = mybir.ActivationFunctionType
AX = mybir.AxisListType

P = 128
J = 8
GROUP = P * J
WIN = 40
BANK = 512
EPS = 1e-5
PER_BANK = 5
TURNS = 4
CHUNK = 500
SCATTER_BANK = 4
PARTS = 3


def node_split(n_nodes):
    parts = max(p for p in range(1, P + 1) if n_nodes % p == 0)
    return parts, n_nodes // parts


def group_count(n_edges):
    return 2 * -(-n_edges // (2 * GROUP))


def program(nc, D, out):
    N, F = D["x"].shape
    PN, C = node_split(N)
    G = D["src"].shape[0]
    PAIRS = G // 2
    F1 = F + 1
    ROUNDS = -(-N // WIN)
    assert C % PER_BANK == 0 and C <= 7 * TURNS and N + WIN <= 8 * BANK and F == 96
    BANKS = C // PER_BANK
    TBANKS = -(-C // TURNS)
    CB = -(-C // 3)
    BLOCK_BANKS = [(c, min(CB, C - c)) for c in range(0, C, CB)]
    BLOCK = C * WIN
    assert CB * WIN <= BANK and BLOCK <= 2048
    STEP = max(k for k in range(1, BANK // WIN + 1) if PAIRS % k == 0)
    STEPS = G // STEP
    assert STEPS % 2 == 0
    CHUNKS = [(k, min(CHUNK, N - k)) for k in range(0, N, CHUNK)]

    table = nc.dram_tensor("table", (N, F), F32, kind="Internal").ap()
    blocks = nc.dram_tensor("blocks", (G, PN, BLOCK), F16, kind="Internal").ap()
    table2 = nc.dram_tensor("table2", (N, 2 * F), F32, kind="Internal").ap()

    ctx = ExitStack()
    with ctx:
        def sb(name, shape, dt=F32):
            return ctx.enter_context(nc.sbuf_tensor(name, shape, dt))

        x = sb("x", [PN, C, F])
        h = sb("h", [PN, C, F])
        t = sb("t", [PN, C, F])
        sq = sb("sq", [PN, C, F])
        store = sb("store", [P, C * 2 * F])
        pre = store[0:PN, :].rearrange("p (c f) -> p c f", c=C)
        hot_cd = store[:, 0:J * BLOCK // 2].bitcast(F16).rearrange("p (j m) -> p j m", j=J)
        parts = store[0:PN, 0:PARTS * C * F // 2].bitcast(BF16).rearrange("p (k c f) -> p k c f", k=PARTS, c=C)
        stat = sb("stat", [PN, C])
        var = sb("var", [PN, C])
        std = sb("std", [PN, C])
        rstd = sb("rstd", [PN, C])
        deg = sb("deg", [PN, C])
        dis = sb("dis", [PN, C])
        featT = sb("featT", [F1, N])
        aggT = sb("aggT", [F1, N + WIN])
        hidT = sb("hidT", [F1, N])
        dst_i = sb("dst_i", [P, G * J], I32)
        dst_f = sb("dst_f", [P, G * J])
        src_i = sb("src_i", [P, G * J], I32)
        src_p = sb("src_p", [P, G * J])
        key = sb("key", [P, G * J])
        rel = sb("rel", [P, G * J])
        bad = sb("bad", [P, G * J])
        wgt = sb("wgt", [P, G * J])
        base_f = sb("base_f", [P, G])
        base_i = sb("base_i", [1, G], I32)
        base_r = sb("base_r", [1, G])
        bad_sum = sb("bad_sum", [P, 1])
        spread = sb("spread", [P, 1])
        fine = sb("fine", [P, 1])
        rounds_f = sb("rounds_f", [1, 1])
        rounds_i = sb("rounds_i", [1, 1], I32)
        idx = [sb(f"idx{b}", [P, J], I32) for b in range(2)]
        rows = [sb(f"rows{b}", [P, J, 2 * F]) for b in range(2)]
        msg = [sb(f"msg{b}", [P, J, F1]) for b in range(2)]
        gat = [sb(f"gat{b}", [P, J, F]) for b in range(2)]
        hot = [sb(f"hot{b}", [P, J, 2 * WIN]) for b in range(2)]
        attr = [sb(f"attr{b}", [P, J * F]) for b in range(2)]
        hot_p = sb("hot_p", [P, J, P], F16)
        block_sb = [sb(f"block{b}", [PN, BLOCK], F16) for b in range(2)]
        step_blocks = [sb(f"step_blocks{b}", [PN, STEP, BLOCK], F16) for b in range(2)]
        logit = [sb(f"logit{b}", [P, J]) for b in range(2)]
        tanh = [sb(f"tanh{b}", [P, J]) for b in range(2)]
        gate = [sb(f"gate{b}", [P, J]) for b in range(2)]
        ident = sb("ident", [P, P])
        ones = sb("ones", [P, P])
        iota = sb("iota", [P, WIN])
        iota_r = sb("iota_r", [P, WIN])
        iota_p = sb("iota_p", [P, P], F16)
        iota_cd = sb("iota_cd", [P, BLOCK], F16)

        def row_consts(name, width, parts=PN):
            return sb(name, [parts, width]), D[name].rearrange("(a f) -> a f", a=1).to_broadcast([parts, width])

        loads = []

        def vector_rows(name, parts=PN):
            tile_, src_ = row_consts(name, D[name].shape[0], parts)
            loads.append((tile_[:], src_))
            return tile_

        def vector_column(name):
            n = D[name].shape[0]
            tile_ = sb("col_" + name, [n, 1])
            loads.append((tile_[:], D[name].rearrange("(f a) -> f a", a=1)))
            return tile_

        def matrix(name, *parts):
            width = sum(D[w].shape[1] for w, _ in parts)
            with_bias = any(b for _, b in parts)
            tile_ = sb(name, [F1 if with_bias else F, width])
            at = 0
            for w, b in parts:
                n = D[w].shape[1]
                loads.append((tile_[0:F, at:at + n], D[w][0:F, :]))
                if b:
                    loads.append((tile_[F:F1, at:at + n], D[b].rearrange("(a f) -> a f", a=1)))
                at += n
            return tile_

        L0_bias, L0_gamma, L0_beta = (vector_rows("L0_gnn_" + k) for k in ("bias", "gamma", "beta"))
        L1_b = [vector_rows(f"L1_gnn_b{k}") for k in range(2)]
        L1_g = [vector_rows(f"L1_gnn_g{k}") for k in range(2)]
        L1_be = [vector_rows(f"L1_gnn_be{k}") for k in range(2)]
        L2_ub2, L2_g, L2_b = (vector_rows("L2_gnn_" + k) for k in ("ub2", "ln_g", "ln_b"))
        L2_ub1 = vector_column("L2_gnn_ub1")
        L3_b1 = vector_column("L3_gnn_b1")
        W0 = sb("W0", [F1, F1])
        loads.append((W0[0:F, 0:F], D["L0_gnn_W"]))
        W1 = [matrix(f"W1_{k}", (f"L1_gnn_W{k}", None)) for k in range(2)]
        W2in = matrix("W2in", ("L2_gnn_mW1", "L2_gnn_mb1"), ("L2_gnn_gW1", "L2_gnn_gb1"))
        W2msg = matrix("W2msg", ("L2_gnn_mW2", "L2_gnn_mb2"))
        W2u_x = sb("W2u_x", [F, F])
        W2u_a = sb("W2u_a", [F, F])
        loads.append((W2u_x[:], D["L2_gnn_uW1"][0:F, :]))
        loads.append((W2u_a[:], D["L2_gnn_uW1"][F:2 * F, :]))
        W2u2 = matrix("W2u2", ("L2_gnn_uW2", None))
        W3pre = matrix("W3pre", ("L3_gnn_W_pre", "L3_gnn_b_pre"))
        W3a = matrix("W3a", ("L3_gnn_W1", None))
        W3b = matrix("W3b", ("L3_gnn_W2", "L3_gnn_b2"))
        ED = D["L2_gnn_mW1"].shape[0] - F
        Q = P // ED
        assert ED == 32
        W2e = sb("W2e", [P, 2 * F])
        for q in range(Q):
            for k, w in enumerate(("L2_gnn_mW1", "L2_gnn_gW1")):
                loads.append((W2e[q * ED:(q + 1) * ED, k * F:(k + 1) * F], D[w][F:F + ED, :]))
        gW2 = sb("gW2", [P, F])
        loads.append((gW2[:], D["L2_gnn_gW2"].rearrange("f a -> a f").to_broadcast([P, F])))
        gb2 = sb("gb2", [P, 1])
        half_gb2 = sb("half_gb2", [P, 1])
        loads.append((gb2[:], D["L2_gnn_gb2"].rearrange("(a f) -> a f", a=1).to_broadcast([P, 1])))

        ps = ctx.enter_context(nc.psum_tensor("ps", [P, 8, BANK], F32))

        def by_tile(T, rows_):
            return T[0:rows_, 0:N].rearrange("f (p c) -> f c p", c=C)

        def banks(width):
            return ps[0:PN, 0:BANKS, 0:PER_BANK * width].rearrange("p b (k m) -> p b k m", m=width)

        def in_banks(T):
            return T.rearrange("p (b k) m -> p b k m", k=PER_BANK)

        def bank_rows(T):
            return T[:].unsqueeze(1).unsqueeze(1).to_broadcast([PN, BANKS, PER_BANK, F])

        def node_rows(T):
            return T[:].unsqueeze(1).to_broadcast([PN, C, F])

        def per_node(T, width=F):
            return T[:].unsqueeze(2).to_broadcast([PN, C, width])

        @contextmanager
        def signals(*names):
            with ExitStack() as s:
                sems = [s.enter_context(nc.semaphore(n)) for n in names]
                yield sems
                for one in sems:
                    nc.sync.sem_clear(one)
                nc.all_engine_barrier(sem_only=True)

        def linker(engine, sem):
            count = [0]

            def link(ins):
                count[0] += 1
                ins.then_inc(sem, 1)
                engine.wait_ge(sem, count[0])
            return link

        def center_scale(dve, link, src, dst, var_ready, std_ready, k):
            link(nc.vector.tensor_reduce(stat[:], src[:], AX.X, ALU.add))
            link(nc.vector.tensor_scalar(stat[:], stat[:], -1.0 / F, None, ALU.mult))
            link(nc.vector.tensor_tensor(dst[:], src[:], per_node(stat), ALU.add))
            link(nc.vector.tensor_tensor(sq[:], dst[:], dst[:], ALU.mult))
            link(nc.vector.tensor_reduce(var[:], sq[:], AX.X, ALU.add))
            nc.vector.tensor_scalar(var[:], var[:], 1.0 / F, EPS, ALU.mult, ALU.add).then_inc(var_ready, 1)
            dve.wait_ge(std_ready, k + 1)
            link(nc.vector.reciprocal(rstd[:], std[:]))
            link(nc.vector.tensor_tensor(dst[:], dst[:], per_node(rstd), ALU.mult))

        def root(act, var_ready, std_ready, k):
            act.wait_ge(var_ready, k + 1)
            nc.scalar.activation(std[:], var[:], ACT.Sqrt).then_inc(std_ready, 1)

        def project(pe, T, rows_, W, width, done):
            tiles = by_tile(T, rows_)
            for c in range(C):
                at = (c % PER_BANK) * width
                mm = pe.matmul(ps[0:PN, c // PER_BANK, at:at + width], tiles[:, c, :], W[0:rows_, 0:width],
                               start=True, stop=True)
            mm.then_inc(done, 1)

        def turn(pe, T, done):
            for c in range(C):
                at = (c % TURNS) * PN
                mm = pe.transpose(ps[0:F, c // TURNS, at:at + PN], T[:, c, :], ident[0:PN, 0:PN])
                if c % TURNS == TURNS - 1 or c == C - 1:
                    mm.then_inc(done, 1)

        def turned(k):
            n = min(TURNS, C - TURNS * k)
            return ps[0:F, k, 0:n * PN].rearrange("f (k p) -> f k p", p=PN)

        def turned_home(T, k):
            return by_tile(T, F)[:, TURNS * k:min(C, TURNS * (k + 1)), :]

        def first_window():
            nc.vector.tensor_copy(iota_r[:], iota[:])
            nc.vector.tensor_copy(base_r[:], base_f[0:1, :])
            nc.vector.tensor_copy(base_i[:], base_f[0:1, :])

        with signals("s_x", "s_dst", "s_loads", "s_zero", "s_const", "s_steps", "s_var", "s_std", "s_h", "s_w0",
                     "s_dstf", "s_base", "s_rel", "s_bad", "s_spread", "s_fine", "s_hgb", "s_src") as S:
            (x_in, dst_in, loaded, zeroed, consts, steps, var_ready, std_ready, h_ready, w0_zero,
             dstf_ready, base_ready, rel_done, bad_ready, spread_ready, stored, hgb, src_in) = S
            with nc.Block() as block:
                @block.sync
                def _(sp):
                    sp.dma_start(x[:], D["x"].rearrange("(p c) f -> p c f", c=C)).then_inc(x_in, 16)
                    sp.dma_start(dst_i[:], D["dst"]).then_inc(dst_in, 16)
                    sp.dma_start(src_i[:], D["src_cols"]).then_inc(src_in, 16)
                    sp.dma_start(wgt[:], D["edge_weight"]).then_inc(loaded, 16)
                    sp.wait_ge(w0_zero, 1)
                    for to, fro in loads:
                        with nc.allow_non_contiguous_dma(reason="columns of biases"):
                            sp.dma_start(to, fro).then_inc(loaded, 16)
                    sp.wait_ge(h_ready, 1)
                    sp.dma_start(table.rearrange("(p c) f -> p c f", c=C), h[:]).then_inc(stored, 16)
                    sp.wait_ge(stored, 16)
                    sp.wait_ge(loaded, 16 * (len(loads) + 1))

                @block.gpsimd
                def _(pool):
                    link = linker(pool, zeroed)
                    link(nc.gpsimd.memset(W0[:], 0.0))
                    nc.gpsimd.memset(W0[F:F1, F:F1], 1.0).then_inc(w0_zero, 1)
                    pool.wait_ge(w0_zero, 1)
                    link(nc.gpsimd.memset(ident[:], 0.0))
                    link(nc.gpsimd.affine_select(out=ident[:], in_=ident[:], compare_op=ALU.not_equal, fill=1.0,
                                                 base=0, pattern=[[-1, P]], channel_multiplier=1))
                    link(nc.gpsimd.memset(ones[:], 1.0))
                    nc.gpsimd.iota(iota[:], [[1, WIN]], base=0, channel_multiplier=0,
                                   allow_small_or_imprecise_dtypes=True).then_inc(consts, 1)
                    pool.wait_ge(consts, 1)
                    link(nc.gpsimd.iota(iota_p[:], [[1, P]], base=0, channel_multiplier=0,
                                        allow_small_or_imprecise_dtypes=True))
                    link(nc.gpsimd.iota(iota_cd[:], [[1, BLOCK]], base=0, channel_multiplier=0,
                                        allow_small_or_imprecise_dtypes=True))
                    link(nc.gpsimd.memset(featT[F:F1, :], 1.0))
                    link(nc.gpsimd.memset(hidT[F:F1, :], 1.0))
                    link(nc.gpsimd.memset(aggT[:], 0.0))
                    for b in range(2):
                        link(nc.gpsimd.memset(msg[b][:, :, F:F1], 1.0))
                        link(nc.gpsimd.memset(rows[b][:, :, F:F1], 1.0))

                @block.tensor
                def _(pe):
                    pe.wait_ge(consts, 1)
                    pe.wait_ge(dstf_ready, 1)
                    pe.matmul(ps[:, 0, 0:G], ones[0:1, :],
                              dst_f[0:1, :].rearrange("p (g j) -> p g j", j=J)[:, :, 0],
                              start=True, stop=True).then_inc(base_ready, 1)
                    pe.wait_ge(bad_ready, 1)
                    pe.matmul(ps[:, 1, 0:1], ones[:], bad_sum[:], start=True, stop=True).then_inc(spread_ready, 1)

                @block.scalar
                def _(act):
                    root(act, var_ready, std_ready, 0)

                @block.vector
                def _(dve):
                    link = linker(dve, steps)
                    dve.wait_ge(x_in, 16)
                    center_scale(dve, link, x, h, var_ready, std_ready, 0)
                    nc.vector.tensor_scalar(h[:], h[:], 0.0, None, ALU.max).then_inc(h_ready, 1)
                    dve.wait_ge(dst_in, 16)
                    nc.vector.tensor_copy(dst_f[:], dst_i[:]).then_inc(dstf_ready, 1)
                    dve.wait_ge(base_ready, 1)
                    dve.wait_ge(dstf_ready, 1)
                    link(nc.vector.tensor_copy(base_f[:], ps[:, 0, 0:G]))
                    grouped = rel[:].rearrange("p (g j) -> p g j", j=J)
                    link(nc.vector.tensor_tensor(grouped, dst_f[:].rearrange("p (g j) -> p g j", j=J),
                                                 base_f[:].unsqueeze(2).to_broadcast([P, G, J]), ALU.subtract))
                    link(nc.vector.tensor_scalar(bad[:], rel[:], 0.0, None, ALU.is_lt))
                    link(nc.vector.scalar_tensor_tensor(out=bad[:], in0=rel[:], scalar=float(WIN), in1=bad[:],
                                                        op0=ALU.is_ge, op1=ALU.max))
                    link(nc.vector.scalar_tensor_tensor(out=bad[:], in0=dst_f[:], scalar=0.0, in1=bad[:],
                                                        op0=ALU.is_ge, op1=ALU.mult))
                    nc.vector.tensor_reduce(bad_sum[:], bad[:], AX.X, ALU.add).then_inc(bad_ready, 1)
                    dve.wait_ge(spread_ready, 1)
                    link(nc.vector.tensor_scalar(fine[:], ps[:, 1, 0:1], 0.5, None, ALU.is_lt))
                    link(nc.vector.tensor_scalar(rounds_f[:], fine[0:1, :], float(1 - ROUNDS), float(ROUNDS),
                                                 ALU.mult, ALU.add))
                    nc.vector.tensor_copy(rounds_i[:], rounds_f[:])
                    link(nc.vector.tensor_scalar(base_f[:], base_f[:], fine[:, 0:1], None, ALU.mult))
                    link(nc.vector.tensor_tensor(grouped, dst_f[:].rearrange("p (g j) -> p g j", j=J),
                                                      base_f[:].unsqueeze(2).to_broadcast([P, G, J]), ALU.subtract))
                    dve.wait_ge(consts, 1)
                    first_window()
                    dve.wait_ge(src_in, 16)
                    link(nc.vector.tensor_copy(key[:], src_i[:]))
                    link(nc.vector.tensor_scalar(bad[:], key[:], 0.5, 1.0 / C, ALU.add, ALU.mult))
                    link(nc.vector.tensor_copy(src_i[:], bad[:]))
                    link(nc.vector.tensor_copy(src_p[:], src_i[:]))
                    link(nc.vector.tensor_tensor(bad[:], src_p[:], bad[:], ALU.is_gt))
                    link(nc.vector.tensor_tensor(src_p[:], src_p[:], bad[:], ALU.subtract))
                    link(nc.vector.scalar_tensor_tensor(out=key[:], in0=src_p[:], scalar=-float(C), in1=key[:],
                                                        op0=ALU.mult, op1=ALU.add))
                    link(nc.vector.scalar_tensor_tensor(out=key[:], in0=key[:], scalar=float(WIN), in1=rel[:],
                                                        op0=ALU.mult, op1=ALU.add))
                    link(nc.vector.tensor_scalar(bad[:], rel[:], 0.0, None, ALU.is_ge))
                    link(nc.vector.scalar_tensor_tensor(out=bad[:], in0=rel[:], scalar=float(WIN), in1=bad[:],
                                                        op0=ALU.is_lt, op1=ALU.mult))
                    link(nc.vector.scalar_tensor_tensor(out=key[:], in0=key[:], scalar=1.0, in1=bad[:],
                                                        op0=ALU.add, op1=ALU.mult))
                    nc.vector.tensor_scalar(key[:], key[:], -1.0, None, ALU.add)
                    dve.wait_ge(loaded, 16 * (len(loads) + 1))
                    nc.vector.tensor_scalar(half_gb2[:], gb2[:], 0.5, None, ALU.mult)

        rounds = nc.values_load(rounds_i[0:1, 0:1], min_val=1, max_val=ROUNDS)

        def edge_pass(layer):
            wide = layer == "L2"
            source = table2 if wide else table
            width = 2 * F if wide else F
            out_rows = F1 if layer in ("L0", "L2") else F
            adds = 2 if layer == "L0" else 1
            takes = {"L0": rows, "L1": rows, "L2": msg, "L3": msg}[layer]
            names = ["idx_in", "attr_in", "gathered", "hot_raw", "hot_ready", "scattered", "added", "rows_used",
                     "mlp_ready", "gate_act", "msg_act", "weighed", "logit_ready", "tanh_ready", "gate_ready",
                     "slot_open", "block_hot", "block_fed", "block_sum", "block_copied", "block_out"]
            with nc.Fori(0, rounds), signals(*[f"s_{n}{b}" for n in names for b in range(2)], "s_moved") as S:
                moved = S[-1]
                (idx_in, attr_in, gathered, hot_raw, hot_ready, scattered, added, rows_used, mlp_ready,
                 gate_act, msg_act, weighed, logit_ready, tanh_ready, gate_ready, slot_open, block_hot, block_fed,
                 block_sum, block_copied, block_out) = (S[2 * k:2 * k + 2]
                                                                                     for k in range(len(names)))

                def free(i):
                    return i + 1

                def done(i):
                    return i + 2

                with nc.Block() as block:
                    @block.sync
                    def _(sp):
                        with sp.Fori(0, PAIRS) as i:
                            for b in range(2):
                                sp.wait_ge((scattered if layer in ("L0", "L1") else rows_used)[b], free(i))
                                sp.dma_start(idx[b][:], D["src"][bass.ds(2 * i + b, 1)].rearrange(
                                    "a p j -> (a p) j")).then_inc(idx_in[b], 16)
                                if layer == "L2":
                                    sp.wait_ge(mlp_ready[b], free(i))
                                    sp.dma_start(attr[b][:, 0:GROUP * ED // P], D["edge_attr_32"][
                                        bass.ds(2 * i + b, 1)].rearrange("a p m -> (a p) m")).then_inc(attr_in[b], 16)
                                if layer == "L3":
                                    sp.wait_ge(rows_used[b], free(i))
                                    sp.dma_start(attr[b][:], D["edge_attr_96"][
                                        bass.ds(2 * i + b, 1)].rearrange("a p m -> (a p) m")).then_inc(attr_in[b], 16)

                    @block.gpsimd
                    def _(pool):
                        with pool.Fori(0, PAIRS) as i:
                            for b in range(2):
                                pool.wait_ge(idx_in[b], 16 * (i + 1))
                                if layer in ("L0", "L1"):
                                    pool.wait_ge(scattered[b], free(i))
                                elif layer == "L2":
                                    pool.wait_ge(msg_act[b], free(i))
                                    pool.wait_ge(gate_act[b], free(i))
                                else:
                                    pool.wait_ge(rows_used[b], free(i))
                                pool.sem_inc(slot_open[b], 1)
                                for j in range(J):
                                    pool.indirect_dma_start(
                                        rows[b][:, j, 0:width], None, source,
                                        bass.IndirectOffsetOnAxis(ap=idx[b][:, j:j + 1], axis=0),
                                    ).then_inc(gathered[b], 16)
                        for b in range(2):
                            pool.wait_ge(gathered[b], 16 * J * PAIRS)
                        for b in range(2):
                            pool.dma_reset(range(gathered[b].num, gathered[b].num + 1))

                    @block.tensor
                    def _(pe):
                        def edge_products(i, b):
                            pe.wait_ge(attr_in[b], 16 * (i + 1))
                            pe.wait_ge(rows_used[1 - b], free(i) if b == 0 else done(i))
                            for k in range(J // Q):
                                for q in range(Q):
                                    mm = pe.matmul(ps[:, q, k * 2 * F:(k + 1) * 2 * F],
                                                   attr[b][q * ED:(q + 1) * ED, k * P:(k + 1) * P],
                                                   W2e[q * ED:(q + 1) * ED, :], start=True, stop=True,
                                                   tile_position=(q * ED, 0))
                            mm.then_inc(mlp_ready[b], 1)

                        def scatter(i, b):
                            if layer in ("L0", "L1"):
                                pe.wait_ge(gathered[b], 16 * J * (i + 1))
                            elif layer == "L2":
                                pe.wait_ge(msg_act[b], done(i))
                            else:
                                pe.wait_ge(rows_used[b], done(i))
                            pe.wait_ge(hot_ready[b], i + 1)
                            pe.wait_ge(added[b], adds * i + 1)
                            cols = 2 * WIN if layer == "L0" else WIN
                            for j in range(J):
                                mm = pe.matmul(ps[0:out_rows, SCATTER_BANK + b, 0:cols], takes[b][:, j, 0:out_rows],
                                               hot[b][:, j, 0:cols], start=(j == 0), stop=(j == J - 1))
                            mm.then_inc(scattered[b], 1)

                        def count_edges(i, b):
                            pe.wait_ge(block_copied[1 - b], free(i) if b == 0 else done(i))
                            for half in range(2):
                                pe.wait_ge(block_hot[half], 2 * i + b + 1)
                                for j in range(half * J // 2, (half + 1) * J // 2):
                                    for k, (c, n) in enumerate(BLOCK_BANKS):
                                        mm = pe.matmul(ps[:, k, 0:n * WIN], hot_p[:, j, :],
                                                       hot_cd[:, j, c * WIN:(c + n) * WIN],
                                                       start=(j == 0), stop=(j == J - 1))
                                mm.then_inc(block_fed[half], 1)

                        for b in range(2):
                            pe.sem_inc(scattered[b], 1)
                            pe.sem_inc(block_fed[b], 1)
                            pe.sem_inc(mlp_ready[b], 1)
                        if layer == "L2":
                            edge_products(0, 0)
                            with pe.Fori(0, PAIRS - 1) as i:
                                edge_products(i, 1)
                                scatter(i, 0)
                                edge_products(i + 1, 0)
                                scatter(i, 1)
                            edge_products(PAIRS - 1, 1)
                            scatter(PAIRS - 1, 0)
                            scatter(PAIRS - 1, 1)
                        else:
                            with pe.Fori(0, PAIRS) as i:
                                for b in range(2):
                                    if layer == "L0":
                                        count_edges(i, b)
                                    scatter(i, b)

                    if layer == "L0":
                        @block.scalar
                        def _(act):
                            for b in range(2):
                                act.sem_inc(block_copied[b], 1)
                            with act.Fori(0, PAIRS) as i:
                                for b in range(2):
                                    act.wait_ge(block_fed[1], 2 * i + b + 2)
                                    for k, (c, n) in enumerate(BLOCK_BANKS):
                                        copied = nc.scalar.copy(block_sb[b][:, c * WIN:(c + n) * WIN],
                                                                ps[0:PN, k, 0:n * WIN])
                                    copied.then_inc(block_copied[b], 1)
                                    act.wait_ge(block_copied[b], done(i))
                                    act.dma_start(blocks[bass.ds(2 * i + b, 1)].rearrange("a p m -> (a p) m"),
                                                  block_sb[b][:]).then_inc(block_out[b], 16)
                                    act.wait_ge(block_out[b], 16 * (i + 1))

                    if layer == "L2":
                        @block.scalar
                        def _(act):
                            for b in range(2):
                                act.sem_inc(gate_act[b], 1)
                                act.sem_inc(msg_act[b], 1)
                            with act.Fori(0, PAIRS) as i:
                                for b in range(2):
                                    act.wait_ge(rows_used[b], done(i))
                                    act.wait_ge(logit_ready[b], free(i))
                                    nc.scalar.activation(gat[b][:], rows[b][:, :, F:2 * F],
                                                         ACT.Gelu).then_inc(gate_act[b], 1)
                                    act.wait_ge(scattered[b], free(i))
                                    nc.scalar.activation(msg[b][:, :, 0:F], rows[b][:, :, 0:F],
                                                         ACT.Gelu).then_inc(msg_act[b], 1)
                                    act.wait_ge(logit_ready[b], done(i))
                                    nc.scalar.activation(tanh[b][:], logit[b][:], ACT.Tanh, bias=half_gb2[:, 0:1],
                                                         scale=0.5).then_inc(tanh_ready[b], 1)

                    @block.vector
                    def _(dve):
                        for b in range(2):
                            dve.sem_inc(rows_used[b], 1)
                            dve.sem_inc(logit_ready[b], 1)
                            dve.sem_inc(added[b], 1)
                        def one_hot(i, b):
                            g = 2 * i + b
                            raw = hot[b][:, :, WIN:2 * WIN] if layer in ("L0", "L2") else hot[b][:, :, 0:WIN]
                            dve.wait_ge(scattered[b], free(i))
                            made = nc.vector.tensor_tensor(
                                raw, rel[:, bass.ds(g * J, J)].unsqueeze(2).to_broadcast([P, J, WIN]),
                                iota_r[:].unsqueeze(1).to_broadcast([P, J, WIN]), ALU.is_equal)
                            if layer in ("L1", "L3"):
                                made.then_inc(hot_ready[b], 1)
                            else:
                                made.then_inc(hot_raw[b], 1)
                            if layer == "L0":
                                dve.wait_ge(hot_raw[b], i + 1)
                                nc.vector.tensor_tensor(
                                    hot[b][:, :, 0:WIN], raw,
                                    wgt[:, bass.ds(g * J, J)].unsqueeze(2).to_broadcast([P, J, WIN]),
                                    ALU.mult).then_inc(hot_ready[b], 1)

                        def block_hots(i, b):
                            g = 2 * i + b
                            for half in range(2):
                                dve.wait_ge(block_fed[half], g + 1)
                                for j in range(half * J // 2, (half + 1) * J // 2):
                                    nc.vector.tensor_scalar(hot_p[:, j, :], iota_p[:],
                                                            src_p[:, bass.ds(g * J + j, 1)], None, ALU.is_equal)
                                    made = nc.vector.tensor_scalar(hot_cd[:, j, :], iota_cd[:],
                                                                   key[:, bass.ds(g * J + j, 1)], None, ALU.is_equal)
                                made.then_inc(block_hot[half], 1)

                        def messages(i, b):
                            dve.wait_ge(gathered[b], 16 * J * (i + 1))
                            dve.wait_ge(attr_in[b], 16 * (i + 1))
                            dve.wait_ge(scattered[b], free(i))
                            nc.vector.tensor_tensor(msg[b][:, :, 0:F], rows[b][:, :, 0:F],
                                                    attr[b][:].rearrange("p (j f) -> p j f", f=F),
                                                    ALU.mult).then_inc(rows_used[b], 1)

                        def hidden(i, b):
                            dve.wait_ge(gathered[b], 16 * J * (i + 1))
                            dve.wait_ge(mlp_ready[b], done(i))
                            sums = rows[b][:].rearrange("p (k q) f -> p q k f", q=Q)
                            prods = ps[:, 0:Q, 0:J // Q * 2 * F].rearrange("p q (k f) -> p q k f", f=2 * F)
                            nc.vector.tensor_tensor(sums, prods, sums, ALU.add).then_inc(rows_used[b], 1)

                        def gates(i, b):
                            dve.wait_ge(gate_act[b], done(i))
                            nc.vector.tensor_tensor(gat[b][:], gat[b][:], gW2[:].unsqueeze(1).to_broadcast([P, J, F]),
                                                    ALU.mult).then_inc(weighed[b], 1)
                            dve.wait_ge(weighed[b], i + 1)
                            nc.vector.tensor_reduce(logit[b][:], gat[b][:], AX.X, ALU.add).then_inc(logit_ready[b], 1)
                            dve.wait_ge(tanh_ready[b], i + 1)
                            nc.vector.tensor_scalar(gate[b][:], tanh[b][:], 0.5, 0.5, ALU.mult,
                                                    ALU.add).then_inc(gate_ready[b], 1)
                            dve.wait_ge(gate_ready[b], i + 1)
                            dve.wait_ge(hot_raw[b], i + 1)
                            nc.vector.tensor_tensor(hot[b][:, :, 0:WIN], hot[b][:, :, WIN:2 * WIN],
                                                    gate[b][:].unsqueeze(2).to_broadcast([P, J, WIN]),
                                                    ALU.mult).then_inc(hot_ready[b], 1)

                        def collect(i, b):
                            first = dve.value_load(base_i[0:1, bass.ds(2 * i + b, 1)], min_val=0, max_val=N)
                            dve.wait_ge(scattered[b], done(i))
                            dve.wait_ge(added[1 - b], adds * i + 1 if b == 0 else adds * (i + 1) + 1)
                            plain_rows = F if layer == "L0" else out_rows
                            home = aggT[0:plain_rows, bass.ds(first, WIN)]
                            nc.vector.tensor_tensor(home, ps[0:plain_rows, SCATTER_BANK + b, 0:WIN], home,
                                                    ALU.add).then_inc(added[b], 1)
                            if layer == "L0":
                                home = aggT[F:F1, bass.ds(first, WIN)]
                                nc.vector.tensor_tensor(home, ps[F:F1, SCATTER_BANK + b, WIN:2 * WIN], home,
                                                        ALU.add).then_inc(added[b], 1)

                        def rest(i, b):
                            one_hot(i, b)
                            if layer == "L0":
                                block_hots(i, b)
                            if layer == "L2":
                                gates(i, b)

                        def first_use(i, b):
                            if layer == "L2":
                                hidden(i, b)
                            if layer == "L3":
                                messages(i, b)

                        first_use(0, 0)
                        rest(0, 0)
                        with dve.Fori(0, PAIRS - 1) as i:
                            first_use(i, 1)
                            collect(i, 0)
                            rest(i, 1)
                            first_use(i + 1, 0)
                            collect(i, 1)
                            rest(i + 1, 0)
                        first_use(PAIRS - 1, 1)
                        collect(PAIRS - 1, 0)
                        rest(PAIRS - 1, 1)
                        collect(PAIRS - 1, 1)
                        nc.vector.tensor_scalar(iota_r[:], iota_r[:], float(WIN), None, ALU.add)
                        nc.vector.tensor_scalar(base_r[:], base_r[:], float(WIN), None,
                                                ALU.add).then_inc(moved, 1)
                        dve.wait_ge(moved, 1)
                        nc.vector.tensor_copy(base_i[:], base_r[:])

        def block_pass():
            names = ["blocks_in", "multiplied"]
            with signals(*[f"s_{n}{b}" for n in names for b in range(2)], "s_summed") as S:
                blocks_in, multiplied, summed = S[0:2], S[2:4], S[4]
                with nc.Block() as block:
                    @block.sync
                    def _(sp):
                        with sp.Fori(0, STEPS // 2) as i:
                            for b in range(2):
                                sp.wait_ge(multiplied[b], i + 1)
                                sp.dma_start(step_blocks[b][:], blocks[bass.ds((2 * i + b) * STEP, STEP)].rearrange(
                                    "g p m -> p g m")).then_inc(blocks_in[b], 16)

                    @block.tensor
                    def _(pe):
                        for b in range(2):
                            pe.sem_inc(multiplied[b], 1)
                        with pe.Fori(0, STEPS // 2) as i:
                            for b in range(2):
                                pe.wait_ge(blocks_in[b], 16 * (i + 1))
                                pe.wait_ge(summed, (2 * i + b + 1) * STEP)
                                step = step_blocks[b][:].rearrange("p g (c d) -> p g c d", d=WIN)
                                for c in range(C):
                                    for k in range(PARTS):
                                        mm = pe.matmul(
                                            ps[0:F, SCATTER_BANK + b, 0:STEP * WIN].rearrange(
                                                "f (g d) -> f g d", d=WIN),
                                            parts[:, k, c, :], step[:, :, c, :],
                                            start=(c == 0 and k == 0), stop=(c == C - 1 and k == PARTS - 1))
                                mm.then_inc(multiplied[b], 1)

                    @block.vector
                    def _(dve):
                        dve.sem_inc(summed, 2 * STEP)
                        with dve.Fori(0, STEPS // 2) as i:
                            for b in range(2):
                                dve.wait_ge(multiplied[b], i + 2)
                                for k in range(STEP):
                                    g = (2 * i + b) * STEP + k
                                    first = dve.value_load(base_i[0:1, bass.ds(g, 1)], min_val=0, max_val=N)
                                    home = aggT[0:F, bass.ds(first, WIN)]
                                    nc.vector.tensor_tensor(home, ps[0:F, SCATTER_BANK + b, k * WIN:(k + 1) * WIN],
                                                            home, ALU.add).then_inc(summed, 1)
                                    dve.wait_ge(summed, g + 2 * STEP + 1)

        def l1_edges():
            with nc.If(rounds < 2):
                block_pass()
            with nc.Else():
                edge_pass("L1")

        def split_table(link):
            link(nc.vector.tensor_copy(parts[:, 0], h[:]))
            link(nc.vector.tensor_tensor(t[:], h[:], parts[:, 0], ALU.subtract))
            link(nc.vector.tensor_copy(parts[:, 1], t[:]))
            link(nc.vector.tensor_tensor(t[:], t[:], parts[:, 1], ALU.subtract))
            link(nc.vector.tensor_copy(parts[:, 2], t[:]))

        def finish_layer_norm(dve, link, gamma, beta):
            link(nc.vector.tensor_tensor(t[:], t[:], node_rows(gamma), ALU.mult))
            link(nc.vector.tensor_tensor(t[:], t[:], node_rows(beta), ALU.add))

        edge_pass("L0")

        with signals("s_proj", "s_steps", "s_var", "s_std", "s_h", "s_turned", "s_deg", "s_sdeg", "s_stored") as S:
            projected, steps, var_ready, std_ready, h_ready, turn_done, deg_ready, sdeg, stored = S
            with nc.Block() as block:
                @block.tensor
                def _(pe):
                    project(pe, aggT, F1, W0, F1, projected)
                    pe.wait_ge(h_ready, 1)
                    turn(pe, h, turn_done)

                @block.scalar
                def _(act):
                    act.wait_ge(deg_ready, 1)
                    nc.scalar.activation(std[:], deg[:], ACT.Sqrt).then_inc(sdeg, 1)
                    root(act, var_ready, std_ready, 0)
                    root(act, var_ready, std_ready, 1)

                @block.vector
                def _(dve):
                    link = linker(dve, steps)
                    dve.wait_ge(projected, 1)
                    nc.vector.tensor_scalar(deg[:].rearrange("p (b k) -> p b k", k=PER_BANK), banks(F1)[:, :, :, F],
                                            1.0, None, ALU.add).then_inc(deg_ready, 1)
                    dve.wait_ge(sdeg, 1)
                    link(nc.vector.reciprocal(dis[:], std[:]))
                    link(nc.vector.tensor_tensor(in_banks(t[:]), banks(F1)[:, :, :, 0:F], bank_rows(L0_bias), ALU.add))
                    center_scale(dve, link, t, t, var_ready, std_ready, 0)
                    finish_layer_norm(dve, link, L0_gamma, L0_beta)
                    link(nc.vector.tensor_tensor(x[:], x[:], t[:], ALU.add))
                    center_scale(dve, link, x, h, var_ready, std_ready, 1)
                    link(nc.vector.tensor_scalar(h[:], h[:], 0.0, None, ALU.max))
                    nc.vector.tensor_tensor(h[:], h[:], per_node(dis), ALU.mult).then_inc(h_ready, 1)
                    dve.wait_ge(h_ready, 1)
                    for k in range(TBANKS):
                        dve.wait_ge(turn_done, k + 1)
                        nc.vector.tensor_copy(turned_home(aggT, k), turned(k))
                    split_table(link)
                    first_window()

                @block.sync
                def _(sp):
                    sp.wait_ge(h_ready, 1)
                    sp.dma_start(table.rearrange("(p c) f -> p c f", c=C), h[:]).then_inc(stored, 16)
                    sp.wait_ge(stored, 16)

        l1_edges()

        def l1_tail(dve, link, k, projected, var_ready, std_ready, z_ready, tanh_done):
            dve.wait_ge(projected, 1)
            nc_dis = dis[:].rearrange("p (b k) -> p b k", k=PER_BANK).unsqueeze(3).to_broadcast(
                [PN, BANKS, PER_BANK, F])
            link(nc.vector.tensor_tensor(in_banks(t[:]), banks(F), nc_dis, ALU.mult))
            nc.vector.tensor_tensor(t[:], t[:], node_rows(L1_b[k]), ALU.add).then_inc(z_ready, 1)
            dve.wait_ge(tanh_done, 1)
            center_scale(dve, link, h, t, var_ready, std_ready, 0)
            finish_layer_norm(dve, link, L1_g[k], L1_be[k])

        with signals("s_proj", "s_steps", "s_var", "s_std", "s_h", "s_turned", "s_z", "s_tanh", "s_stored") as S:
            projected, steps, var_ready, std_ready, h_ready, turn_done, z_ready, tanh_done, stored = S
            with nc.Block() as block:
                @block.tensor
                def _(pe):
                    project(pe, aggT, F, W1[0], F, projected)
                    pe.wait_ge(h_ready, 1)
                    turn(pe, h, turn_done)

                @block.scalar
                def _(act):
                    act.wait_ge(z_ready, 1)
                    nc.scalar.activation(h[:], t[:], ACT.Tanh).then_inc(tanh_done, 1)
                    root(act, var_ready, std_ready, 0)

                @block.vector
                def _(dve):
                    link = linker(dve, steps)
                    l1_tail(dve, link, 0, projected, var_ready, std_ready, z_ready, tanh_done)
                    nc.vector.tensor_tensor(h[:], t[:], per_node(dis), ALU.mult).then_inc(h_ready, 1)
                    dve.wait_ge(h_ready, 1)
                    for k in range(TBANKS):
                        dve.wait_ge(turn_done, k + 1)
                        nc.vector.tensor_copy(turned_home(aggT, k), turned(k))
                    split_table(link)
                    first_window()

                @block.sync
                def _(sp):
                    sp.wait_ge(h_ready, 1)
                    sp.dma_start(table.rearrange("(p c) f -> p c f", c=C), h[:]).then_inc(stored, 16)
                    sp.wait_ge(stored, 16)

        l1_edges()

        PRE_TILES = 8
        PRE_STEPS = [(k, min(PRE_TILES, C - k)) for k in range(0, C, PRE_TILES)]
        with signals("s_proj", "s_steps", "s_var", "s_std", "s_h", "s_turned", "s_z", "s_tanh", "s_feat", "s_pre",
                     "s_pret", "s_stored") as S:
            (projected, steps, var_ready, std_ready, h_ready, turn_done, z_ready, tanh_done, feat_ready, pre_done,
             pre_taken, stored) = S
            with nc.Block() as block:
                @block.tensor
                def _(pe):
                    project(pe, aggT, F, W1[1], F, projected)
                    pe.wait_ge(h_ready, 1)
                    turn(pe, h, turn_done)
                    pe.wait_ge(feat_ready, TBANKS)
                    tiles = by_tile(featT, F1)
                    for s, (c0, n) in enumerate(PRE_STEPS):
                        if s >= 2:
                            pe.wait_ge(pre_taken, s - 1)
                        for c in range(c0, c0 + n):
                            k = c - c0
                            mm = pe.matmul(ps[0:PN, 4 * (s % 2) + k // 2, (k % 2) * 2 * F:(k % 2 + 1) * 2 * F],
                                           tiles[:, c, :], W2in[:], start=True, stop=True)
                        mm.then_inc(pre_done, 1)

                @block.scalar
                def _(act):
                    act.wait_ge(z_ready, 1)
                    nc.scalar.activation(h[:], t[:], ACT.Tanh).then_inc(tanh_done, 1)
                    root(act, var_ready, std_ready, 0)
                    root(act, var_ready, std_ready, 1)

                @block.vector
                def _(dve):
                    link = linker(dve, steps)
                    l1_tail(dve, link, 1, projected, var_ready, std_ready, z_ready, tanh_done)
                    link(nc.vector.tensor_tensor(x[:], x[:], t[:], ALU.add))
                    center_scale(dve, link, x, h, var_ready, std_ready, 1)
                    nc.vector.tensor_scalar(h[:], h[:], 0.0, None, ALU.max).then_inc(h_ready, 1)
                    for k in range(TBANKS):
                        dve.wait_ge(turn_done, k + 1)
                        nc.vector.tensor_copy(turned_home(featT, k), turned(k)).then_inc(feat_ready, 1)
                    first_window()
                    nc.vector.memset(aggT[:], 0.0)
                    for s, (c0, n) in enumerate(PRE_STEPS):
                        dve.wait_ge(pre_done, s + 1)
                        for k in range(0, n, 2):
                            m = min(2, n - k)
                            last = nc.vector.tensor_copy(
                                pre[:, c0 + k:c0 + k + m, :],
                                ps[0:PN, 4 * (s % 2) + k // 2, 0:m * 2 * F].rearrange("p (k f) -> p k f", k=m))
                        last.then_inc(pre_taken, 1)

                @block.sync
                def _(sp):
                    sp.wait_ge(pre_taken, len(PRE_STEPS))
                    sp.dma_start(table2.rearrange("(p c) f -> p c f", c=C), pre[:]).then_inc(stored, 16)
                    sp.wait_ge(stored, 16)

        edge_pass("L2")

        with signals("s_agg", "s_aggt", "s_hid", "s_hidt", "s_proj", "s_steps", "s_var", "s_std", "s_h", "s_turned",
                     "s_feat", "s_pre", "s_tab", "s_stored") as S:
            (agg_done, agg_taken, hid_done, hid_taken, projected, steps, var_ready, std_ready, h_ready, turn_done,
             feat_ready, pre_done, table_ready, stored) = S
            with nc.Block() as block:
                @block.tensor
                def _(pe):
                    for n, (at, w) in enumerate(CHUNKS):
                        pe.matmul(ps[0:F, n, 0:w], W2msg[:], aggT[0:F1, at:at + w], start=True,
                                  stop=True).then_inc(agg_done, 1)
                    for n, (at, w) in enumerate(CHUNKS):
                        pe.wait_ge(agg_taken, n + 1)
                        pe.matmul(ps[0:F, n, 0:w], W2u_x[:], featT[0:F, at:at + w], start=True, stop=False)
                        pe.matmul(ps[0:F, n, 0:w], W2u_a[:], aggT[0:F, at:at + w], start=False,
                                  stop=True).then_inc(hid_done, 1)
                    pe.wait_ge(hid_taken, len(CHUNKS))
                    project(pe, hidT, F, W2u2, F, projected)
                    pe.wait_ge(h_ready, 1)
                    turn(pe, h, turn_done)
                    pe.wait_ge(feat_ready, TBANKS)
                    project(pe, featT, F1, W3pre, F, pre_done)

                @block.scalar
                def _(act):
                    for n, (at, w) in enumerate(CHUNKS):
                        act.wait_ge(hid_done, n + 1)
                        nc.scalar.activation(hidT[0:F, at:at + w], ps[0:F, n, 0:w], ACT.Gelu,
                                             bias=L2_ub1[:, 0:1]).then_inc(hid_taken, 1)
                    root(act, var_ready, std_ready, 0)
                    root(act, var_ready, std_ready, 1)
                    act.wait_ge(pre_done, 1)
                    nc.scalar.activation(in_banks(t[:]), banks(F), ACT.Gelu).then_inc(table_ready, 1)

                @block.vector
                def _(dve):
                    link = linker(dve, steps)
                    for n, (at, w) in enumerate(CHUNKS):
                        dve.wait_ge(agg_done, n + 1)
                        nc.vector.tensor_copy(aggT[0:F, at:at + w], ps[0:F, n, 0:w]).then_inc(agg_taken, 1)
                    dve.wait_ge(projected, 1)
                    link(nc.vector.tensor_tensor(in_banks(t[:]), banks(F), bank_rows(L2_ub2), ALU.add))
                    link(nc.vector.tensor_tensor(t[:], t[:], h[:], ALU.add))
                    center_scale(dve, link, t, t, var_ready, std_ready, 0)
                    finish_layer_norm(dve, link, L2_g, L2_b)
                    link(nc.vector.tensor_tensor(x[:], x[:], t[:], ALU.add))
                    center_scale(dve, link, x, h, var_ready, std_ready, 1)
                    nc.vector.tensor_scalar(h[:], h[:], 0.0, None, ALU.max).then_inc(h_ready, 1)
                    for k in range(TBANKS):
                        dve.wait_ge(turn_done, k + 1)
                        nc.vector.tensor_copy(turned_home(featT, k), turned(k)).then_inc(feat_ready, 1)
                    first_window()
                    nc.vector.memset(aggT[:], 0.0)

                @block.sync
                def _(sp):
                    sp.wait_ge(table_ready, 1)
                    sp.dma_start(table.rearrange("(p c) f -> p c f", c=C), t[:]).then_inc(stored, 16)
                    sp.wait_ge(stored, 16)

        edge_pass("L3")

        with signals("s_sum", "s_hid", "s_hidt", "s_proj", "s_xt", "s_y", "s_xd", "s_steps", "s_out", "s_stored") as S:
            sum_ready, hid_done, hid_taken, projected, x_turned, y_ready, x_taken, steps, out_ready, stored = S
            with nc.Block() as block:
                @block.tensor
                def _(pe):
                    for n, (at, w) in enumerate(CHUNKS):
                        pe.wait_ge(sum_ready, n + 1)
                        pe.matmul(ps[0:F, n, 0:w], W3a[:], aggT[0:F, at:at + w], start=True,
                                  stop=True).then_inc(hid_done, 1)
                    pe.wait_ge(hid_taken, len(CHUNKS))
                    project(pe, hidT, F1, W3b, F, projected)
                    pe.wait_ge(y_ready, 1)
                    project(pe, aggT, F, ident, F, x_turned)

                @block.scalar
                def _(act):
                    for n, (at, w) in enumerate(CHUNKS):
                        act.wait_ge(hid_done, n + 1)
                        nc.scalar.activation(hidT[0:F, at:at + w], ps[0:F, n, 0:w], ACT.Gelu,
                                             bias=L3_b1[:, 0:1]).then_inc(hid_taken, 1)
                    act.wait_ge(projected, 1)
                    nc.scalar.activation(in_banks(t[:]), banks(F), ACT.Gelu).then_inc(y_ready, 1)

                @block.vector
                def _(dve):
                    link = linker(dve, steps)
                    for n, (at, w) in enumerate(CHUNKS):
                        nc.vector.tensor_tensor(aggT[0:F, at:at + w], featT[0:F, at:at + w], aggT[0:F, at:at + w],
                                                ALU.add).then_inc(sum_ready, 1)
                    dve.wait_ge(y_ready, 1)
                    link(nc.vector.tensor_tensor(x[:], x[:], t[:], ALU.add))
                    dve.wait_ge(x_turned, 1)
                    nc.vector.tensor_tensor(in_banks(x[:]), banks(F), in_banks(x[:]), ALU.add).then_inc(out_ready, 1)

                @block.sync
                def _(sp):
                    sp.wait_ge(out_ready, 1)
                    sp.dma_start(out.rearrange("(p c) f -> p c f", c=C), x[:]).then_inc(stored, 16)
                    sp.wait_ge(stored, 16)


def kernel(**inputs):
    import numpy as _np
    import concourse.bacc as _bacc
    from concourse import mybir as _mybir
    from concourse.bass_utils import run_bass_kernel_spmd as _run

    arrays = {k: _np.asarray(v) for k, v in inputs.items()}
    n_edges = arrays["src"].shape[0]
    groups = group_count(n_edges)

    def padded(a, fill):
        full = _np.full((groups * GROUP,) + a.shape[1:], fill, a.dtype)
        full[:n_edges] = a
        return full

    arrays["src"] = padded(arrays["src"], 0).reshape(groups, P, J)
    arrays["src_cols"] = arrays["src"].transpose(1, 0, 2).reshape(P, groups * J)
    for name, fill in (("dst", -1), ("edge_weight", 0)):
        arrays[name] = padded(arrays[name], fill).reshape(groups, P, J).transpose(1, 0, 2).reshape(P, groups * J)
    arrays["edge_attr_96"] = padded(arrays["edge_attr_96"], 0).reshape(groups, P, -1)
    a = padded(arrays["edge_attr_32"], 0)
    f = a.shape[1]
    q = P // f
    arrays["edge_attr_32"] = a.reshape(groups, P, J // q, q, f).transpose(0, 3, 4, 2, 1).reshape(groups, P, -1)

    nc = _bacc.Bacc("TRN2", target_bir_lowering=False, num_devices=1)
    feeds, D = {}, {}
    for name, a in arrays.items():
        a = _np.ascontiguousarray(a)
        feeds[f"in_{name}"] = a
        D[name] = nc.dram_tensor(f"in_{name}", a.shape, _mybir.dt.from_np(a.dtype), kind="ExternalInput").ap()
    out = nc.dram_tensor("out_x", inputs["x"].shape, F32, kind="ExternalOutput").ap()
    program(nc, D, out)
    r = _run(nc, [feeds], core_ids=[0])
    return r.results[0]["out_x"]
```

```python
import math
from contextlib import ExitStack, contextmanager

import concourse.bass as bass
from concourse import mybir

F32 = mybir.dt.float32
F16 = mybir.dt.float16
I32 = mybir.dt.int32
ALU = mybir.AluOpType
ACT = mybir.ActivationFunctionType
AX = mybir.AxisListType

P = 128
J = 8
GROUP = P * J
WIN = 40
BANK = 512
EPS = 1e-5
PER_BANK = 5
TURNS = 4
CHUNK = 500
SCATTER_BANK = 4
PARTS = 2
PICK_BANK = 6
HALF_MAX = 65504.0
PAIR_BITS = 12
PAIR_BASE = 1 << PAIR_BITS
PICKED = {"L0": (1, 0), "L1": (0, 0), "L2": (0, 0), "L3": (2, 2)}


def node_split(n_nodes):
    parts = max(p for p in range(1, P + 1) if n_nodes % p == 0)
    return parts, n_nodes // parts


def group_count(n_edges):
    return 2 * -(-n_edges // (2 * GROUP))


def program(nc, D, out):
    N, F = D["x"].shape
    PN, C = node_split(N)
    G = D["src"].shape[0]
    PAIRS = G // 2
    F1 = F + 1
    ROUNDS = -(-N // WIN)
    assert C % PER_BANK == 0 and C <= 7 * TURNS and N + WIN <= 8 * BANK and F == 96
    BANKS = C // PER_BANK
    TBANKS = -(-C // TURNS)
    CB = -(-C // 3)
    BLOCK_BANKS = [(c, min(CB, C - c)) for c in range(0, C, CB)]
    BLOCK = C * WIN
    assert CB * WIN <= BANK and BLOCK <= 2048
    STEP = max(k for k in range(1, BANK // WIN + 1) if PAIRS % k == 0)
    STEPS = G // STEP
    assert STEPS % 2 == 0
    MOST_PICKED = max(max(n) for n in PICKED.values())
    assert C * MOST_PICKED * P <= STEP * BLOCK
    assert N < PAIR_BASE and N * (PAIR_BASE + 1) < 1 << 24
    CHUNKS = [(k, min(CHUNK, N - k)) for k in range(0, N, CHUNK)]

    ROOT_F = math.sqrt(F)
    NORM_SCALE = 2.0 ** math.floor(math.log2(HALF_MAX / ROOT_F))
    BOUND_SCALE = 2.0 ** 14

    table = nc.dram_tensor("table", (N, F), F32, kind="Internal").ap()
    blocks = nc.dram_tensor("blocks", (G, PN, BLOCK), F16, kind="Internal").ap()
    table2 = nc.dram_tensor("table2", (N, 2 * F), F32, kind="Internal").ap()

    ctx = ExitStack()
    with ctx:
        def sb(name, shape, dt=F32):
            return ctx.enter_context(nc.sbuf_tensor(name, shape, dt))

        x = sb("x", [PN, C, F])
        h = sb("h", [PN, C, F])
        t = sb("t", [PN, C, F])
        x_beta = sb("x_beta", [PN, C, F])
        assert 2 * G * J <= C * 2 * F
        store = sb("store", [P, C * 2 * F])
        pre = store[0:PN, :].rearrange("p (c f) -> p c f", c=C)
        hot_cd = store[:, 0:J * BLOCK // 2].bitcast(F16).rearrange("p (j m) -> p j m", j=J)
        parts = store[0:PN, 0:PARTS * C * F // 2].bitcast(F16).rearrange("p (c f) -> p c f", c=C)
        first_parts = t[:].rearrange("p c f -> p (c f)").bitcast(F16).rearrange("p (c f) -> p c f", c=C)
        bad = store[:, 0:G * J]
        halves = sb("halves", [PN, C, 6])
        neg_mean = sb("neg_mean", [PN, C])
        apart = sb("apart", [PN, C])
        scale = sb("scale", [PN, C])
        shift = sb("shift", [PN, C])
        var = sb("var", [PN, C])
        std = sb("std", [PN, C])
        rstd = sb("rstd", [PN, C])
        deg = sb("deg", [PN, C])
        dis = sb("dis", [PN, C])
        featT = sb("featT", [F1, N])
        aggT = sb("aggT", [F1, N + WIN])
        hidT = sb("hidT", [F1, N])
        dst_i = sb("dst_i", [P, G * J], I32)
        dst_f = sb("dst_f", [P, G * J])
        src_f = dst_f
        src_i = sb("src_i", [P, G * J], I32)
        src_p = sb("src_p", [P, G * J])
        key = sb("key", [P, G * J])
        rel = sb("rel", [P, G * J])
        wgt = sb("wgt", [P, G * J])
        base_f = sb("base_f", [P, G])
        pair_f = sb("pair_f", [1, PAIRS])
        pair_r = sb("pair_r", [1, PAIRS])
        pair_i = sb("pair_i", [1, PAIRS], I32)
        bad_sum = sb("bad_sum", [P, 1])
        spread = sb("spread", [P, 1])
        fine = sb("fine", [P, 1])
        rounds_f = sb("rounds_f", [1, 1])
        rounds_i = sb("rounds_i", [1, 1], I32)
        idx = [sb(f"idx{b}", [P, J], I32) for b in range(2)]
        rows = [sb(f"rows{b}", [P, J, 2 * F]) for b in range(2)]
        msg = [sb(f"msg{b}", [P, J, F1]) for b in range(2)]
        gat = [sb(f"gat{b}", [P, J, F]) for b in range(2)]
        hot = [sb(f"hot{b}", [P, J, 2 * WIN]) for b in range(2)]
        attr = [sb(f"attr{b}", [P, J * F]) for b in range(2)]
        hot_p = sb("hot_p", [P, J, P], F16)
        block_sb = [sb(f"block{b}", [PN, BLOCK], F16) for b in range(2)]
        step_blocks = [sb(f"step_blocks{b}", [PN, STEP, BLOCK], F16) for b in range(2)]
        src_row = [sb(f"src_row{b}", [PN, MOST_PICKED * P], I32) for b in range(2)]
        src_rel = [sb(f"src_rel{b}", [PN, MOST_PICKED * P], F16) for b in range(2)]
        pick_hot = [step_blocks[b][:].rearrange("p g m -> p (g m)") for b in range(2)]
        logit = [sb(f"logit{b}", [P, J]) for b in range(2)]
        tanh = [sb(f"tanh{b}", [P, J]) for b in range(2)]
        gate = [sb(f"gate{b}", [P, J]) for b in range(2)]
        ident = sb("ident", [P, P])
        ones = sb("ones", [P, P])
        iota = sb("iota", [P, WIN])
        iota_r = sb("iota_r", [P, WIN])
        iota_p = sb("iota_p", [P, P], F16)
        iota_cd = sb("iota_cd", [P, BLOCK], F16)
        first_src = sb("first_src", [P, 1])
        bound = [sb(f"bound{k}", [PN, F]) for k in range(2)]
        power = [sb(f"power{k}", [PN, F]) for k in range(2)]
        unpower = [sb(f"unpower{k}", [PN, F]) for k in range(2)]
        unscale = [sb(f"unscale{k}", [F, 1]) for k in range(2)]
        abs_pre = sb("abs_pre", [F1, F])
        L1_g_scaled = sb("L1_g_scaled", [PN, F])
        L1_be_scaled = sb("L1_be_scaled", [PN, F])
        W1_scaled = sb("W1_scaled", [F, F])

        def row_consts(name, width, parts=PN):
            return sb(name, [parts, width]), D[name].rearrange("(a f) -> a f", a=1).to_broadcast([parts, width])

        loads = []

        def vector_rows(name, parts=PN):
            tile_, src_ = row_consts(name, D[name].shape[0], parts)
            loads.append((tile_[:], src_))
            return tile_

        def vector_column(name):
            n = D[name].shape[0]
            tile_ = sb("col_" + name, [n, 1])
            loads.append((tile_[:], D[name].rearrange("(f a) -> f a", a=1)))
            return tile_

        def matrix(name, *parts):
            width = sum(D[w].shape[1] for w, _ in parts)
            with_bias = any(b for _, b in parts)
            tile_ = sb(name, [F1 if with_bias else F, width])
            at = 0
            for w, b in parts:
                n = D[w].shape[1]
                loads.append((tile_[0:F, at:at + n], D[w][0:F, :]))
                if b:
                    loads.append((tile_[F:F1, at:at + n], D[b].rearrange("(a f) -> a f", a=1)))
                at += n
            return tile_

        L0_bias, L0_gamma, L0_beta = (vector_rows("L0_gnn_" + k) for k in ("bias", "gamma", "beta"))
        L1_b = [vector_rows(f"L1_gnn_b{k}") for k in range(2)]
        L1_g = [vector_rows(f"L1_gnn_g{k}") for k in range(2)]
        L1_be = [vector_rows(f"L1_gnn_be{k}") for k in range(2)]
        L2_g, L2_b = (vector_rows("L2_gnn_" + k) for k in ("ln_g", "ln_b"))
        L2_ub1 = vector_column("L2_gnn_ub1")
        L3_b1 = vector_column("L3_gnn_b1")
        W0 = sb("W0", [F1, F1])
        loads.append((W0[0:F, 0:F], D["L0_gnn_W"]))
        W1 = [matrix(f"W1_{k}", (f"L1_gnn_W{k}", None)) for k in range(2)]
        W2in = matrix("W2in", ("L2_gnn_mW1", "L2_gnn_mb1"), ("L2_gnn_gW1", "L2_gnn_gb1"))
        W2msg = matrix("W2msg", ("L2_gnn_mW2", "L2_gnn_mb2"))
        W2u_x = sb("W2u_x", [F, F])
        W2u_a = sb("W2u_a", [F, F])
        loads.append((W2u_x[:], D["L2_gnn_uW1"][0:F, :]))
        loads.append((W2u_a[:], D["L2_gnn_uW1"][F:2 * F, :]))
        W2msg_T = sb("W2msg_T", [F, F1])
        W2agg = sb("W2agg", [F1, F])
        W2u2 = matrix("W2u2", ("L2_gnn_uW2", "L2_gnn_ub2"))
        W3pre = matrix("W3pre", ("L3_gnn_W_pre", "L3_gnn_b_pre"))
        W3a = matrix("W3a", ("L3_gnn_W1", None))
        W3b = matrix("W3b", ("L3_gnn_W2", "L3_gnn_b2"))
        ED = D["L2_gnn_mW1"].shape[0] - F
        Q = P // ED
        assert ED == 32
        W2e = sb("W2e", [P, 2 * F])
        for q in range(Q):
            for k, w in enumerate(("L2_gnn_mW1", "L2_gnn_gW1")):
                loads.append((W2e[q * ED:(q + 1) * ED, k * F:(k + 1) * F], D[w][F:F + ED, :]))
        gW2 = sb("gW2", [P, F])
        loads.append((gW2[:], D["L2_gnn_gW2"].rearrange("f a -> a f").to_broadcast([P, F])))
        gb2 = sb("gb2", [P, 1])
        half_gb2 = sb("half_gb2", [P, 1])
        loads.append((gb2[:], D["L2_gnn_gb2"].rearrange("(a f) -> a f", a=1).to_broadcast([P, 1])))

        ps = ctx.enter_context(nc.psum_tensor("ps", [P, 8, BANK], F32))

        def by_tile(T, rows_):
            return T[0:rows_, 0:N].rearrange("f (p c) -> f c p", c=C)

        def banks(width):
            return ps[0:PN, 0:BANKS, 0:PER_BANK * width].rearrange("p b (k m) -> p b k m", m=width)

        def in_banks(T):
            return T.rearrange("p (b k) m -> p b k m", k=PER_BANK)

        def bank_rows(T):
            return T[:].unsqueeze(1).to_broadcast([PN, PER_BANK, F])

        def node_rows(T):
            return T[:].unsqueeze(1).to_broadcast([PN, C, F])

        def per_node(T, width=F):
            return T[:].unsqueeze(2).to_broadcast([PN, C, width])

        @contextmanager
        def signals(*names):
            with ExitStack() as s:
                sems = [s.enter_context(nc.semaphore(n)) for n in names]
                yield sems
                numbers = {one.num for one in sems}
                for first in sorted(n for n in numbers if n - 1 not in numbers):
                    end = min(n for n in range(first, first + len(numbers) + 1) if n not in numbers)
                    nc.sync.sem_clear(range(first, end))
                nc.all_engine_barrier(sem_only=True)

        def linker(engine, sem):
            count = [0]

            def link(ins):
                count[0] += 1
                ins.then_inc(sem, 1)
                engine.wait_ge(sem, count[0])
            return link

        def statistics(dve, link, src, var_ready, std_ready, k):
            for c in range(C):
                last = nc.vector.bn_stats(halves[:, c, :], src(c))
            link(last)
            link(nc.vector.tensor_tensor(apart[:], halves[:, :, 1], halves[:, :, 4], ALU.subtract))
            nc.vector.tensor_tensor(var[:], halves[:, :, 2], halves[:, :, 5], ALU.add)
            link(nc.vector.scalar_tensor_tensor(out=apart[:], in0=apart[:], scalar=0.25, in1=apart[:],
                                                op0=ALU.mult, op1=ALU.mult))
            link(nc.vector.tensor_scalar(apart[:], apart[:], EPS, None, ALU.add))
            nc.vector.scalar_tensor_tensor(out=var[:], in0=var[:], scalar=1.0 / F, in1=apart[:],
                                           op0=ALU.mult, op1=ALU.add).then_inc(var_ready, 1)
            link(nc.vector.tensor_tensor(neg_mean[:], halves[:, :, 1], halves[:, :, 4], ALU.add))
            link(nc.vector.tensor_scalar(neg_mean[:], neg_mean[:], -0.5, None, ALU.mult))
            dve.wait_ge(std_ready, k + 1)
            link(nc.vector.reciprocal(rstd[:], std[:]))

        def normalize(link, src, dst):
            for c in range(C):
                last = nc.vector.tensor_scalar(dst[:, c, :], src(c), neg_mean[:, c:c + 1], rstd[:, c:c + 1],
                                               ALU.add, ALU.mult)
            link(last)

        ACT_TILES = C * 8 // 25

        def normalize_relu(link, factor, with_dis, scale_ready, done_):
            if with_dis:
                link(nc.vector.scalar_tensor_tensor(out=scale[:], in0=rstd[:], scalar=factor, in1=dis[:],
                                                    op0=ALU.mult, op1=ALU.mult))
            else:
                link(nc.vector.tensor_scalar(scale[:], rstd[:], factor, None, ALU.mult))
            nc.vector.tensor_tensor(shift[:], neg_mean[:], scale[:], ALU.mult).then_inc(scale_ready, 1)
            for c in range(C - ACT_TILES):
                last = nc.vector.tensor_scalar(h[:, c, :], x[:, c, :], neg_mean[:, c:c + 1], 0.0, ALU.add, ALU.max)
            link(last)
            for c in range(C - ACT_TILES):
                last = nc.vector.tensor_scalar(h[:, c, :], h[:, c, :], scale[:, c:c + 1], None, ALU.mult)
            last.then_inc(done_, 1)

        def normalize_relu_act(act, scale_ready, done_):
            act.wait_ge(scale_ready, 1)
            for c in range(C - ACT_TILES, C):
                last = nc.scalar.activation(h[:, c, :], x[:, c, :], ACT.Relu, bias=shift[:, c:c + 1],
                                            scale=scale[:, c:c + 1])
            last.then_inc(done_, 1)

        def root(act, var_ready, std_ready, k):
            act.wait_ge(var_ready, k + 1)
            nc.scalar.activation(std[:], var[:], ACT.Sqrt).then_inc(std_ready, 1)

        def project(pe, T, rows_, W, width, done):
            tiles = by_tile(T, rows_)
            for c in range(C):
                at = (c % PER_BANK) * width
                mm = pe.matmul(ps[0:PN, c // PER_BANK, at:at + width], tiles[:, c, :], W[0:rows_, 0:width],
                               start=True, stop=True)
                if c % PER_BANK == PER_BANK - 1:
                    mm.then_inc(done, 1)

        def turn(pe, T, done):
            for c in range(C):
                at = (c % TURNS) * PN
                mm = pe.transpose(ps[0:F, c // TURNS, at:at + PN], T[:, c, :], ident[0:PN, 0:PN])
                if c % TURNS == TURNS - 1 or c == C - 1:
                    mm.then_inc(done, 1)

        def turned(k):
            n = min(TURNS, C - TURNS * k)
            return ps[0:F, k, 0:n * PN].rearrange("f (k p) -> f k p", p=PN)

        def turned_home(T, k):
            return by_tile(T, F)[:, TURNS * k:min(C, TURNS * (k + 1)), :]

        def first_window():
            nc.vector.tensor_copy(iota_r[:], iota[:])
            nc.vector.tensor_copy(pair_r[:], pair_f[:])
            nc.vector.tensor_copy(pair_i[:], pair_f[:])

        def first_nodes(dve, i):
            both = dve.value_load(pair_i[0:1, bass.ds(i, 1)], min_val=0, max_val=N * (PAIR_BASE + 1))
            return ((both & (PAIR_BASE - 1)).with_bounds(min_val=0, max_val=N), (both >> PAIR_BITS).with_bounds(min_val=0, max_val=N))

        def split_table(link, source, to):
            link(nc.vector.tensor_copy(to[:, :, 0:F], source[:]))
            link(nc.vector.tensor_tensor(to[:, :, F:2 * F], source[:], to[:, :, 0:F], ALU.subtract))

        with signals("s_x", "s_dst", "s_loads", "s_zero", "s_const", "s_steps", "s_var", "s_std", "s_h", "s_w0",
                     "s_dstf", "s_base", "s_bad", "s_spread", "s_stored", "s_src", "s_scale") as S:
            (x_in, dst_in, loaded, zeroed, consts, steps, var_ready, std_ready, h_ready, w0_zero,
             dstf_ready, base_ready, bad_ready, spread_ready, stored, src_in, scale_ready) = S
            with nc.Block() as block:
                @block.sync
                def _(sp):
                    sp.dma_start(x[:], D["x"].rearrange("(p c) f -> p c f", c=C)).then_inc(x_in, 16)
                    sp.dma_start(dst_i[:], D["dst"]).then_inc(dst_in, 16)
                    sp.dma_start(src_i[:], D["src_cols"]).then_inc(src_in, 16)
                    sp.dma_start(wgt[:], D["edge_weight"]).then_inc(loaded, 16)
                    sp.wait_ge(w0_zero, 1)
                    for to, fro in loads:
                        with nc.allow_non_contiguous_dma(reason="columns of biases"):
                            sp.dma_start(to, fro).then_inc(loaded, 16)
                    sp.wait_ge(h_ready, 2)
                    sp.dma_start(table.rearrange("(p c) f -> p c f", c=C), h[:]).then_inc(stored, 16)
                    sp.wait_ge(stored, 16)
                    sp.wait_ge(loaded, 16 * (len(loads) + 1))

                @block.gpsimd
                def _(pool):
                    link = linker(pool, zeroed)
                    link(nc.gpsimd.memset(W0[:], 0.0))
                    nc.gpsimd.memset(W0[F:F1, F:F1], 1.0).then_inc(w0_zero, 1)
                    pool.wait_ge(w0_zero, 1)
                    link(nc.gpsimd.memset(ident[:], 0.0))
                    link(nc.gpsimd.affine_select(out=ident[:], in_=ident[:], compare_op=ALU.not_equal, fill=1.0,
                                                 base=0, pattern=[[-1, P]], channel_multiplier=1))
                    link(nc.gpsimd.memset(ones[:], 1.0))
                    nc.gpsimd.iota(iota[:], [[1, WIN]], base=0, channel_multiplier=0,
                                   allow_small_or_imprecise_dtypes=True).then_inc(consts, 1)
                    pool.wait_ge(consts, 1)
                    link(nc.gpsimd.iota(iota_p[:], [[1, P]], base=0, channel_multiplier=0,
                                        allow_small_or_imprecise_dtypes=True))
                    link(nc.gpsimd.iota(iota_cd[:], [[1, BLOCK]], base=1, channel_multiplier=0,
                                        allow_small_or_imprecise_dtypes=True))
                    link(nc.gpsimd.iota(first_src[:], [[1, 1]], base=0, channel_multiplier=C,
                                        allow_small_or_imprecise_dtypes=True))
                    link(nc.gpsimd.memset(featT[F:F1, :], 1.0))
                    link(nc.gpsimd.memset(hidT[F:F1, :], 1.0))
                    link(nc.gpsimd.memset(aggT[:], 0.0))
                    for b in range(2):
                        link(nc.gpsimd.memset(msg[b][:, :, F:F1], 1.0))
                        link(nc.gpsimd.memset(rows[b][:, :, F:F1], 1.0))

                @block.tensor
                def _(pe):
                    pe.wait_ge(consts, 1)
                    pe.wait_ge(dstf_ready, 1)
                    pe.matmul(ps[:, 0, 0:G], ones[0:1, :],
                              dst_f[0:1, :].rearrange("p (g j) -> p g j", j=J)[:, :, 0],
                              start=True, stop=True).then_inc(base_ready, 1)
                    pe.wait_ge(bad_ready, 1)
                    pe.matmul(ps[:, 1, 0:1], ones[:], bad_sum[:], start=True, stop=True).then_inc(spread_ready, 1)

                @block.scalar
                def _(act):
                    root(act, var_ready, std_ready, 0)
                    normalize_relu_act(act, scale_ready, h_ready)

                @block.vector
                def _(dve):
                    link = linker(dve, steps)
                    dve.wait_ge(x_in, 16)
                    statistics(dve, link, lambda c: x[:, c, :], var_ready, std_ready, 0)
                    normalize_relu(link, NORM_SCALE, False, scale_ready, h_ready)
                    dve.wait_ge(dst_in, 16)
                    nc.vector.tensor_copy(dst_f[:], dst_i[:]).then_inc(dstf_ready, 1)
                    dve.wait_ge(base_ready, 1)
                    dve.wait_ge(dstf_ready, 1)
                    link(nc.vector.tensor_copy(base_f[:], ps[:, 0, 0:G]))
                    grouped = rel[:].rearrange("p (g j) -> p g j", j=J)
                    link(nc.vector.tensor_tensor(grouped, dst_f[:].rearrange("p (g j) -> p g j", j=J),
                                                 base_f[:].unsqueeze(2).to_broadcast([P, G, J]), ALU.subtract))
                    link(nc.vector.tensor_scalar(bad, rel[:], 0.0, None, ALU.is_lt))
                    link(nc.vector.scalar_tensor_tensor(out=bad, in0=rel[:], scalar=float(WIN), in1=bad,
                                                        op0=ALU.is_ge, op1=ALU.max))
                    link(nc.vector.scalar_tensor_tensor(out=bad, in0=dst_f[:], scalar=0.0, in1=bad,
                                                        op0=ALU.is_ge, op1=ALU.mult))
                    nc.vector.tensor_reduce(bad_sum[:], bad, AX.X, ALU.add).then_inc(bad_ready, 1)
                    dve.wait_ge(spread_ready, 1)
                    link(nc.vector.tensor_scalar(fine[:], ps[:, 1, 0:1], 0.5, None, ALU.is_lt))
                    link(nc.vector.tensor_scalar(rounds_f[:], fine[0:1, :], float(1 - ROUNDS), float(ROUNDS),
                                                 ALU.mult, ALU.add))
                    nc.vector.tensor_copy(rounds_i[:], rounds_f[:])
                    link(nc.vector.tensor_scalar(base_f[:], base_f[:], fine[:, 0:1], None, ALU.mult))
                    link(nc.vector.tensor_tensor(grouped, dst_f[:].rearrange("p (g j) -> p g j", j=J),
                                                      base_f[:].unsqueeze(2).to_broadcast([P, G, J]), ALU.subtract))
                    bases = base_f[0:1, :].rearrange("p (i b) -> p i b", b=2)
                    link(nc.vector.scalar_tensor_tensor(out=pair_f[:], in0=bases[:, :, 1], scalar=float(PAIR_BASE),
                                                        in1=bases[:, :, 0], op0=ALU.mult, op1=ALU.add))
                    dve.wait_ge(consts, 1)
                    first_window()
                    dve.wait_ge(src_in, 16)
                    dve.wait_ge(loaded, 16 * (len(loads) + 1))
                    nc.vector.tensor_scalar(half_gb2[:], gb2[:], 0.5, None, ALU.mult)
                    nc.vector.tensor_scalar(W0[0:F, 0:F], W0[0:F, 0:F], 1.0 / NORM_SCALE, None, ALU.mult)
                    nc.vector.tensor_scalar(W1[0][:], W1[0][:], 1.0 / NORM_SCALE, None, ALU.mult)
                    nc.vector.tensor_copy(src_f[:], src_i[:])

        rounds = nc.values_load(rounds_i[0:1, 0:1], min_val=1, max_val=ROUNDS)

        def prepare_keys(link):
            quotient, rounded = store[:, 0:G * J], store[:, G * J:2 * G * J].bitcast(I32)
            link(nc.vector.tensor_scalar(quotient, src_f[:], 0.5, 1.0 / C, ALU.add, ALU.mult))
            link(nc.vector.tensor_copy(rounded, quotient))
            link(nc.vector.tensor_copy(src_p[:], rounded))
            link(nc.vector.tensor_tensor(quotient, src_p[:], quotient, ALU.is_gt))
            link(nc.vector.tensor_tensor(src_p[:], src_p[:], quotient, ALU.subtract))
            link(nc.vector.scalar_tensor_tensor(out=key[:], in0=src_p[:], scalar=-float(C), in1=src_f[:],
                                                op0=ALU.mult, op1=ALU.add))
            link(nc.vector.scalar_tensor_tensor(out=key[:], in0=key[:], scalar=float(WIN), in1=rel[:],
                                                op0=ALU.mult, op1=ALU.add))
            link(nc.vector.tensor_scalar(key[:], key[:], 1.0, None, ALU.add))
            link(nc.vector.scalar_tensor_tensor(out=key[:], in0=rel[:], scalar=0.0, in1=key[:],
                                                op0=ALU.is_ge, op1=ALU.mult))

        def prepare_scales(dve, link, abs_ready, bound_ready, power_ready, powers_turned):
            def absolute(to, source):
                return nc.vector.scalar_tensor_tensor(out=to[:], in0=source[:], scalar=-1.0, in1=source[:],
                                                      op0=ALU.mult, op1=ALU.max)

            absolute(abs_pre, W3pre).then_inc(abs_ready, 1)
            link(absolute(bound[0], L1_g[0]))
            link(absolute(power[0], L1_be[0]))
            link(nc.vector.scalar_tensor_tensor(out=bound[0][:], in0=bound[0][:], scalar=ROOT_F,
                                                in1=power[0][:], op0=ALU.mult, op1=ALU.add))
            dve.wait_ge(bound_ready, 1)
            link(nc.vector.tensor_scalar(bound[1][:], ps[0:PN, 6, 0:F], ROOT_F, None, ALU.mult))
            for k in range(2):
                link(nc.vector.tensor_scalar(bound[k][:], bound[k][:], 2.0 ** -60, None, ALU.max))
                link(nc.vector.tensor_scalar(unpower[k][:].bitcast(I32), bound[k][:].bitcast(I32),
                                             0x7F800000, None, ALU.bitwise_and))
                link(nc.vector.tensor_scalar(unpower[k][:], unpower[k][:], 1.0 / BOUND_SCALE, None, ALU.mult))
                last = nc.vector.reciprocal(power[k][:], unpower[k][:])
            link(last)
            dve.sem_inc(power_ready, 1)
            nc.vector.tensor_tensor(L1_g_scaled[:], L1_g[0][:], power[0][:], ALU.mult)
            nc.vector.tensor_tensor(L1_be_scaled[:], L1_be[0][:], power[0][:], ALU.mult)
            dve.wait_ge(powers_turned, 1)
            for k in range(2):
                last = nc.vector.tensor_copy(unscale[k][:], ps[0:F, 7, k:k + 1])
            link(last)
            nc.vector.tensor_scalar(W1_scaled[:], W1[1][:], unscale[0][:, 0:1], None, ALU.mult)

        def sum_and_turn_scales(pe, abs_ready, bound_ready, power_ready, powers_turned):
            pe.wait_ge(abs_ready, 1)
            pe.matmul(ps[0:PN, 6, 0:F], ones[0:F1, 0:PN], abs_pre[:], start=True, stop=True).then_inc(bound_ready, 1)
            pe.wait_ge(power_ready, 1)
            for k in range(2):
                mm = pe.matmul(ps[0:F, 7, k:k + 1], unpower[k][0:1, :], ones[0:1, 0:1], start=True, stop=True)
            mm.then_inc(powers_turned, 1)

        def edge_pass(layer):
            wide = layer == "L2"
            source = table2 if wide else table
            width = 2 * F if wide else F
            out_rows = F1 if layer in ("L0", "L2") else F
            adds = 2 if layer == "L0" else 1
            takes = {"L0": rows, "L1": rows, "L2": msg, "L3": msg}[layer]
            names = ["idx_in", "attr_in", "gathered", "hot_raw", "hot_ready", "scattered", "added", "rows_used",
                     "mlp_ready", "gate_act", "msg_act", "weighed", "logit_ready", "tanh_ready", "gate_ready",
                     "slot_open", "block_hot", "block_fed", "block_sum", "block_copied", "block_out",
                     "src_row_in", "centred", "pick_ready", "picked", "high_taken", "rows_picked"]
            picks = PICKED[layer]
            pick_parts = first_parts if layer == "L0" else parts
            with nc.Fori(0, rounds), signals(*[f"s_{n}{b}" for n in names for b in range(2)], "s_moved", "s_prepared", "s_abs",
                                                "s_bound", "s_power", "s_turned") as S:
                moved, prepared, scale_signals = S[-6], S[-5], S[-4:]
                (idx_in, attr_in, gathered, hot_raw, hot_ready, scattered, added, rows_used, mlp_ready,
                 gate_act, msg_act, weighed, logit_ready, tanh_ready, gate_ready, slot_open, block_hot, block_fed,
                 block_sum, block_copied, block_out, src_row_in, centred, pick_ready, picked,
                 high_taken, rows_picked) = (S[2 * k:2 * k + 2] for k in range(len(names)))

                def free(i):
                    return i + 1

                def done(i):
                    return i + 2

                with nc.Block() as block:
                    @block.sync
                    def _(sp):
                        with sp.Fori(0, PAIRS) as i:
                            for b in range(2):
                                if picks[b]:
                                    sp.wait_ge(centred[b], free(i))
                                    sp.dma_start(src_row[b][:, 0:picks[b] * P], D["src_tiles"][
                                        bass.ds(2 * i + b, 1), 0:picks[b] * P].to_broadcast(
                                        [PN, picks[b] * P])).then_inc(src_row_in[b], 16)
                                sp.wait_ge((scattered if layer in ("L0", "L1") else rows_used)[b], free(i))
                                sp.dma_start(idx[b][:], D["src"][bass.ds(2 * i + b, 1)].rearrange(
                                    "a p j -> (a p) j")).then_inc(idx_in[b], 16)
                                if layer == "L2":
                                    sp.wait_ge(mlp_ready[b], free(i))
                                    sp.dma_start(attr[b][:, 0:GROUP * ED // P], D["edge_attr_32"][
                                        bass.ds(2 * i + b, 1)].rearrange("a p m -> (a p) m")).then_inc(attr_in[b], 16)
                                if layer == "L3":
                                    sp.wait_ge(rows_used[b], free(i))
                                    sp.dma_start(attr[b][:], D["edge_attr_96"][
                                        bass.ds(2 * i + b, 1)].rearrange("a p m -> (a p) m")).then_inc(attr_in[b], 16)

                    @block.gpsimd
                    def _(pool):
                        with pool.Fori(0, PAIRS) as i:
                            for b in range(2):
                                pool.wait_ge(idx_in[b], 16 * (i + 1))
                                if layer in ("L0", "L1"):
                                    pool.wait_ge(scattered[b], free(i))
                                elif layer == "L2":
                                    pool.wait_ge(msg_act[b], free(i))
                                    pool.wait_ge(gate_act[b], free(i))
                                else:
                                    pool.wait_ge(rows_used[b], free(i))
                                pool.sem_inc(slot_open[b], 1)
                                for j in range(picks[b], J):
                                    pool.indirect_dma_start(
                                        rows[b][:, j, 0:width], None, source,
                                        bass.IndirectOffsetOnAxis(ap=idx[b][:, j:j + 1], axis=0),
                                    ).then_inc(gathered[b], 16)
                        for b in range(2):
                            pool.wait_ge(gathered[b], 16 * (J - picks[b]) * PAIRS)
                        for b in range(2):
                            pool.dma_reset(range(gathered[b].num, gathered[b].num + 1))

                    @block.tensor
                    def _(pe):
                        def edge_products(i, b):
                            pe.wait_ge(attr_in[b], 16 * (i + 1))
                            pe.wait_ge(rows_used[1 - b], free(i) if b == 0 else done(i))
                            for k in range(J // Q):
                                for q in range(Q):
                                    mm = pe.matmul(ps[:, q, k * 2 * F:(k + 1) * 2 * F],
                                                   attr[b][q * ED:(q + 1) * ED, k * P:(k + 1) * P],
                                                   W2e[q * ED:(q + 1) * ED, :], start=True, stop=True,
                                                   tile_position=(q * ED, 0))
                            mm.then_inc(mlp_ready[b], 1)

                        def pick(i, b):
                            if not picks[b]:
                                return
                            """Rows of the group's first tiles: one-hots of src times the table's parts, side by side."""
                            pe.wait_ge(pick_ready[b], i + 1)
                            pe.wait_ge(rows_picked[b], free(i))
                            for j in range(picks[b]):
                                for c in range(C):
                                    at = c * picks[b] * P + j * P
                                    mm = pe.matmul(ps[:, PICK_BANK + b, j * PARTS * F:(j + 1) * PARTS * F],
                                                   pick_hot[b][:, at:at + P], pick_parts[:, c, :],
                                                   start=(c == 0), stop=(c == C - 1))
                            mm.then_inc(picked[b], 1)

                        def scatter(i, b):
                            if picks[b]:
                                pe.wait_ge(rows_picked[b], done(i))
                            if layer in ("L0", "L1"):
                                pe.wait_ge(gathered[b], 16 * (J - picks[b]) * (i + 1))
                            elif layer == "L2":
                                pe.wait_ge(msg_act[b], done(i))
                            else:
                                pe.wait_ge(rows_used[b], done(i))
                            pe.wait_ge(hot_ready[b], i + 1)
                            pe.wait_ge(added[b], adds * i + 1)
                            cols = 2 * WIN if layer == "L0" else WIN
                            for j in range(J):
                                mm = pe.matmul(ps[0:out_rows, SCATTER_BANK + b, 0:cols], takes[b][:, j, 0:out_rows],
                                               hot[b][:, j, 0:cols], start=(j == 0), stop=(j == J - 1))
                            mm.then_inc(scattered[b], 1)

                        def count_edges(i, b):
                            pe.wait_ge(block_copied[1 - b], free(i) if b == 0 else done(i))
                            for half in range(2):
                                pe.wait_ge(block_hot[half], 2 * i + b + 1)
                                for j in range(half * J // 2, (half + 1) * J // 2):
                                    for k, (c, n) in enumerate(BLOCK_BANKS):
                                        mm = pe.matmul(ps[:, k, 0:n * WIN], hot_p[:, j, :],
                                                       hot_cd[:, j, c * WIN:(c + n) * WIN],
                                                       start=(j == 0), stop=(j == J - 1))
                                mm.then_inc(block_fed[half], 1)

                        for b in range(2):
                            pe.sem_inc(scattered[b], 1)
                            pe.sem_inc(block_fed[b], 1)
                            pe.sem_inc(mlp_ready[b], 1)
                            pe.sem_inc(picked[b], 1)
                        if layer == "L0":
                            sum_and_turn_scales(pe, *scale_signals)
                        if layer == "L2":
                            edge_products(0, 0)
                            with pe.Fori(0, PAIRS - 1) as i:
                                edge_products(i, 1)
                                scatter(i, 0)
                                edge_products(i + 1, 0)
                                scatter(i, 1)
                            edge_products(PAIRS - 1, 1)
                            scatter(PAIRS - 1, 0)
                            scatter(PAIRS - 1, 1)
                        elif layer == "L0" or any(picks):
                            def sums(i, b):
                                scatter(i, b)
                                if layer == "L0":
                                    count_edges(i, b)

                            pick(0, 0)
                            with pe.Fori(0, PAIRS - 1) as i:
                                pick(i, 1)
                                sums(i, 0)
                                pick(i + 1, 0)
                                sums(i, 1)
                            pick(PAIRS - 1, 1)
                            sums(PAIRS - 1, 0)
                            sums(PAIRS - 1, 1)
                        else:
                            with pe.Fori(0, PAIRS) as i:
                                for b in range(2):
                                    scatter(i, b)

                    def picked_part(b, k):
                        return ps[:, PICK_BANK + b, 0:picks[b] * PARTS * F].rearrange(
                            "p (j k f) -> p j k f", j=picks[b], k=PARTS)[:, :, k, :]

                    if layer == "L0" or any(picks):
                        @block.scalar
                        def _(act):
                            def take_high(i, b):
                                if not picks[b]:
                                    return
                                """The picked rows' first parts; DVE adds the second ones."""
                                act.wait_ge(picked[b], done(i))
                                act.wait_ge((scattered if layer == "L0" else rows_used)[b], free(i))
                                nc.scalar.copy(rows[b][:, 0:picks[b], 0:F], picked_part(b, 0)).then_inc(high_taken[b], 1)

                            def store_block(i, b):
                                act.wait_ge(block_fed[1], 2 * i + b + 2)
                                act.wait_ge(block_out[b], 16 * (i + 1))
                                for k, (c, n) in enumerate(BLOCK_BANKS):
                                    copied = nc.scalar.copy(block_sb[b][:, c * WIN:(c + n) * WIN],
                                                            ps[0:PN, k, 0:n * WIN])
                                copied.then_inc(block_copied[b], 1)
                                act.wait_ge(block_copied[b], done(i))
                                act.dma_start(blocks[bass.ds(2 * i + b, 1)].rearrange("a p m -> (a p) m"),
                                              block_sb[b][:]).then_inc(block_out[b], 16)

                            for b in range(2):
                                act.sem_inc(block_copied[b], 1)
                                act.sem_inc(block_out[b], 16)
                            take_high(0, 0)
                            with act.Fori(0, PAIRS - 1) as i:
                                take_high(i, 1)
                                if layer == "L0":
                                    store_block(i, 0)
                                take_high(i + 1, 0)
                                if layer == "L0":
                                    store_block(i, 1)
                            take_high(PAIRS - 1, 1)
                            if layer == "L0":
                                for b in range(2):
                                    store_block(PAIRS - 1, b)
                                for b in range(2):
                                    act.wait_ge(block_out[b], 16 * (PAIRS + 1))

                    if layer == "L2":
                        @block.scalar
                        def _(act):
                            for b in range(2):
                                act.sem_inc(gate_act[b], 1)
                                act.sem_inc(msg_act[b], 1)
                            with act.Fori(0, PAIRS) as i:
                                for b in range(2):
                                    act.wait_ge(rows_used[b], done(i))
                                    act.wait_ge(logit_ready[b], free(i))
                                    nc.scalar.activation(gat[b][:], rows[b][:, :, F:2 * F],
                                                         ACT.Gelu).then_inc(gate_act[b], 1)
                                    act.wait_ge(scattered[b], free(i))
                                    nc.scalar.activation(msg[b][:, :, 0:F], rows[b][:, :, 0:F],
                                                         ACT.Gelu).then_inc(msg_act[b], 1)
                                    act.wait_ge(logit_ready[b], done(i))
                                    nc.scalar.activation(tanh[b][:], logit[b][:], ACT.Tanh, bias=half_gb2[:, 0:1],
                                                         scale=0.5).then_inc(tanh_ready[b], 1)

                    @block.vector
                    def _(dve):
                        for b in range(2):
                            dve.sem_inc(rows_used[b], 1)
                            dve.sem_inc(logit_ready[b], 1)
                            dve.sem_inc(added[b], 1)
                            dve.sem_inc(centred[b], 1)
                            dve.sem_inc(rows_picked[b], 1)

                        def pick_hots(i, b):
                            if not picks[b]:
                                return
                            """One-hots of src for the tiles that PE picks, [p, c, edge]: src - C p is c."""
                            dve.wait_ge(src_row_in[b], 16 * (i + 1))
                            nc.vector.tensor_scalar(src_rel[b][:, 0:picks[b] * P], src_row[b][:, 0:picks[b] * P],
                                                    first_src[0:PN, 0:1], None,
                                                    ALU.subtract).then_inc(centred[b], 1)
                            dve.wait_ge(centred[b], done(i))
                            dve.wait_ge(picked[b], free(i))
                            for c in range(C):
                                made = nc.vector.tensor_scalar(
                                    pick_hot[b][:, c * picks[b] * P:(c + 1) * picks[b] * P], src_rel[b][:, 0:picks[b] * P],
                                    float(c), None, ALU.is_equal)
                            made.then_inc(pick_ready[b], 1)

                        def take_picked(i, b):
                            dve.wait_ge(high_taken[b], i + 1)
                            nc.vector.tensor_tensor(rows[b][:, 0:picks[b], 0:F], picked_part(b, 1),
                                                    rows[b][:, 0:picks[b], 0:F], ALU.add).then_inc(rows_picked[b], 1)

                        def one_hot(i, b):
                            g = 2 * i + b
                            raw = hot[b][:, :, WIN:2 * WIN] if layer in ("L0", "L2") else hot[b][:, :, 0:WIN]
                            dve.wait_ge(scattered[b], free(i))
                            made = nc.vector.tensor_tensor(
                                raw, rel[:, bass.ds(g * J, J)].unsqueeze(2).to_broadcast([P, J, WIN]),
                                iota_r[:].unsqueeze(1).to_broadcast([P, J, WIN]), ALU.is_equal)
                            if layer in ("L1", "L3"):
                                made.then_inc(hot_ready[b], 1)
                            else:
                                made.then_inc(hot_raw[b], 1)
                            if layer == "L0":
                                dve.wait_ge(hot_raw[b], i + 1)
                                nc.vector.tensor_tensor(
                                    hot[b][:, :, 0:WIN], raw,
                                    wgt[:, bass.ds(g * J, J)].unsqueeze(2).to_broadcast([P, J, WIN]),
                                    ALU.mult).then_inc(hot_ready[b], 1)

                        def block_hots(i, b):
                            g = 2 * i + b
                            for half in range(2):
                                dve.wait_ge(block_fed[half], g + 1)
                                for j in range(half * J // 2, (half + 1) * J // 2):
                                    nc.vector.tensor_scalar(hot_p[:, j, :], iota_p[:],
                                                            src_p[:, bass.ds(g * J + j, 1)], None, ALU.is_equal)
                                    made = nc.vector.tensor_scalar(hot_cd[:, j, :], iota_cd[:],
                                                                   key[:, bass.ds(g * J + j, 1)], None, ALU.is_equal)
                                made.then_inc(block_hot[half], 1)

                        def messages(i, b):
                            dve.wait_ge(rows_picked[b], done(i))
                            dve.wait_ge(gathered[b], 16 * (J - picks[b]) * (i + 1))
                            dve.wait_ge(attr_in[b], 16 * (i + 1))
                            dve.wait_ge(scattered[b], free(i))
                            nc.vector.tensor_tensor(msg[b][:, :, 0:F], rows[b][:, :, 0:F],
                                                    attr[b][:].rearrange("p (j f) -> p j f", f=F),
                                                    ALU.mult).then_inc(rows_used[b], 1)

                        def hidden(i, b):
                            dve.wait_ge(gathered[b], 16 * (J - picks[b]) * (i + 1))
                            dve.wait_ge(mlp_ready[b], done(i))
                            sums = rows[b][:].rearrange("p (k q) f -> p q k f", q=Q)
                            prods = ps[:, 0:Q, 0:J // Q * 2 * F].rearrange("p q (k f) -> p q k f", f=2 * F)
                            nc.vector.tensor_tensor(sums, prods, sums, ALU.add).then_inc(rows_used[b], 1)

                        def gates(i, b):
                            dve.wait_ge(gate_act[b], done(i))
                            nc.vector.tensor_tensor(gat[b][:], gat[b][:], gW2[:].unsqueeze(1).to_broadcast([P, J, F]),
                                                    ALU.mult).then_inc(weighed[b], 1)
                            dve.wait_ge(weighed[b], i + 1)
                            nc.vector.tensor_reduce(logit[b][:], gat[b][:], AX.X, ALU.add).then_inc(logit_ready[b], 1)
                            dve.wait_ge(tanh_ready[b], i + 1)
                            nc.vector.tensor_scalar(gate[b][:], tanh[b][:], 0.5, 0.5, ALU.mult,
                                                    ALU.add).then_inc(gate_ready[b], 1)
                            dve.wait_ge(gate_ready[b], i + 1)
                            dve.wait_ge(hot_raw[b], i + 1)
                            nc.vector.tensor_tensor(hot[b][:, :, 0:WIN], hot[b][:, :, WIN:2 * WIN],
                                                    gate[b][:].unsqueeze(2).to_broadcast([P, J, WIN]),
                                                    ALU.mult).then_inc(hot_ready[b], 1)

                        def collect(i, b, first):
                            dve.wait_ge(scattered[b], done(i))
                            dve.wait_ge(added[1 - b], adds * i + 1 if b == 0 else adds * (i + 1) + 1)
                            plain_rows = F if layer == "L0" else out_rows
                            home = aggT[0:plain_rows, bass.ds(first, WIN)]
                            nc.vector.tensor_tensor(home, ps[0:plain_rows, SCATTER_BANK + b, 0:WIN], home,
                                                    ALU.add).then_inc(added[b], 1)
                            if layer == "L0":
                                home = aggT[F:F1, bass.ds(first, WIN)]
                                nc.vector.tensor_tensor(home, ps[F:F1, SCATTER_BANK + b, WIN:2 * WIN], home,
                                                        ALU.add).then_inc(added[b], 1)

                        def rest(i, b):
                            one_hot(i, b)
                            if layer == "L0":
                                block_hots(i, b)
                            if layer == "L2":
                                gates(i, b)

                        def first_use(i, b):
                            if picks[b]:
                                take_picked(i, b)
                            if layer == "L2":
                                hidden(i, b)
                            if layer == "L3":
                                messages(i, b)

                        def step(i, b, last_i, next_i, last_first):
                            if next_i is not None:
                                pick_hots(next_i, 1 - b)
                            first_use(i, b)
                            if layer in ("L2", "L3"):
                                collect(last_i, 1 - b, last_first)
                                rest(i, b)
                            else:
                                rest(i, b)
                                collect(last_i, 1 - b, last_first)

                        if layer == "L0":
                            link = linker(dve, prepared)
                            split_table(link, h, first_parts)
                            prepare_keys(link)
                            prepare_scales(dve, link, *scale_signals)
                        pick_hots(0, 0)
                        pick_hots(0, 1)
                        first_use(0, 0)
                        rest(0, 0)
                        with dve.Fori(0, PAIRS - 1) as i:
                            firsts = first_nodes(dve, i)
                            step(i, 1, i, i + 1, firsts[0])
                            step(i + 1, 0, i, i + 1, firsts[1])
                        firsts = first_nodes(dve, PAIRS - 1)
                        step(PAIRS - 1, 1, PAIRS - 1, None, firsts[0])
                        collect(PAIRS - 1, 1, firsts[1])
                        nc.vector.tensor_scalar(iota_r[:], iota_r[:], float(WIN), None, ALU.add)
                        nc.vector.tensor_scalar(pair_r[:], pair_r[:], float(WIN * (PAIR_BASE + 1)), None,
                                                ALU.add).then_inc(moved, 1)
                        dve.wait_ge(moved, 1)
                        nc.vector.tensor_copy(pair_i[:], pair_r[:])

        def block_pass():
            names = ["blocks_in", "multiplied"]
            with signals(*[f"s_{n}{b}" for n in names for b in range(2)], "s_summed") as S:
                blocks_in, multiplied, summed = S[0:2], S[2:4], S[4]
                with nc.Block() as block:
                    @block.sync
                    def _(sp):
                        with sp.Fori(0, STEPS // 2) as i:
                            for b in range(2):
                                sp.wait_ge(multiplied[b], i + 1)
                                sp.dma_start(step_blocks[b][:], blocks[bass.ds((2 * i + b) * STEP, STEP)].rearrange(
                                    "g p m -> p g m")).then_inc(blocks_in[b], 16)

                    @block.tensor
                    def _(pe):
                        for b in range(2):
                            pe.sem_inc(multiplied[b], 1)
                        with pe.Fori(0, STEPS // 2) as i:
                            for b in range(2):
                                pe.wait_ge(blocks_in[b], 16 * (i + 1))
                                pe.wait_ge(summed, (2 * i + b + 1) * STEP)
                                step = step_blocks[b][:].rearrange("p g (c d) -> p g c d", d=WIN)
                                for c in range(C):
                                    for k in range(PARTS):
                                        mm = pe.matmul(
                                            ps[0:F, SCATTER_BANK + b, 0:STEP * WIN].rearrange(
                                                "f (g d) -> f g d", d=WIN),
                                            parts[:, c, k * F:(k + 1) * F], step[:, :, c, :],
                                            start=(c == 0 and k == 0), stop=(c == C - 1 and k == PARTS - 1))
                                mm.then_inc(multiplied[b], 1)

                    @block.vector
                    def _(dve):
                        dve.sem_inc(summed, 2 * STEP)
                        with dve.Fori(0, STEPS // 2) as i:
                            firsts = [n for k in range(STEP) for n in first_nodes(dve, i * STEP + k)]
                            for b in range(2):
                                dve.wait_ge(multiplied[b], i + 2)
                                for k in range(STEP):
                                    g = (2 * i + b) * STEP + k
                                    home = aggT[0:F, bass.ds(firsts[b * STEP + k], WIN)]
                                    nc.vector.tensor_tensor(home, ps[0:F, SCATTER_BANK + b, k * WIN:(k + 1) * WIN],
                                                            home, ALU.add).then_inc(summed, 1)
                                    dve.wait_ge(summed, g + 2 * STEP + 1)

        def l1_edges():
            with nc.If(rounds < 2):
                block_pass()
            with nc.Else():
                edge_pass("L1")

        def add_beta(beta, done_):
            nc.gpsimd.tensor_tensor(x_beta[:], x[:], node_rows(beta), ALU.add).then_inc(done_, 1)

        def take_turned(act, T, turn_done, done_=None):
            for k in range(TBANKS):
                act.wait_ge(turn_done, k + 1)
                copied = nc.scalar.copy(turned_home(T, k), turned(k))
                if done_ is not None:
                    copied.then_inc(done_, 1)

        edge_pass("L0")

        with signals("s_proj", "s_steps", "s_var", "s_std", "s_h", "s_turned", "s_deg", "s_sdeg",
                     "s_wturn", "s_wtaken", "s_wprod", "s_beta", "s_scale", "s_stored") as S:
            (projected, steps, var_ready, std_ready, h_ready, turn_done, deg_ready, sdeg, w_turned,
             w_taken, w_product, beta_ready, scale_ready, stored) = S
            with nc.Block() as block:
                @block.tensor
                def _(pe):
                    project(pe, aggT, F1, W0, F1, projected)
                    pe.transpose(ps[0:F, 7, 0:F1], W2msg[:], ident[0:F1, 0:F1]).then_inc(w_turned, 1)
                    pe.wait_ge(w_taken, 1)
                    pe.matmul(ps[0:F1, 7, 0:F], W2msg_T[:], W2u_a[:], start=True, stop=True).then_inc(w_product, 1)
                    pe.wait_ge(h_ready, 2)
                    turn(pe, h, turn_done)

                @block.scalar
                def _(act):
                    act.wait_ge(deg_ready, 1)
                    nc.scalar.activation(std[:], deg[:], ACT.Sqrt).then_inc(sdeg, 1)
                    act.wait_ge(w_turned, 1)
                    nc.scalar.copy(W2msg_T[:], ps[0:F, 7, 0:F1]).then_inc(w_taken, 1)
                    act.wait_ge(w_product, 1)
                    nc.scalar.copy(W2agg[:], ps[0:F1, 7, 0:F])
                    root(act, var_ready, std_ready, 0)
                    root(act, var_ready, std_ready, 1)
                    normalize_relu_act(act, scale_ready, h_ready)
                    take_turned(act, aggT, turn_done)

                @block.gpsimd
                def _(pool):
                    add_beta(L0_beta, beta_ready)

                @block.vector
                def _(dve):
                    link = linker(dve, steps)
                    for b in range(BANKS):
                        dve.wait_ge(projected, b + 1)
                        last = nc.vector.tensor_tensor(in_banks(t[:])[:, b], banks(F1)[:, b, :, 0:F],
                                                       bank_rows(L0_bias), ALU.add)
                    link(last)
                    nc.vector.tensor_scalar(deg[:].rearrange("p (b k) -> p b k", k=PER_BANK), banks(F1)[:, :, :, F],
                                            1.0, None, ALU.add).then_inc(deg_ready, 1)
                    dve.wait_ge(sdeg, 1)
                    link(nc.vector.reciprocal(dis[:], std[:]))
                    statistics(dve, link, lambda c: t[:, c, :], var_ready, std_ready, 0)
                    normalize(link, lambda c: t[:, c, :], t)
                    link(nc.vector.tensor_tensor(t[:], t[:], node_rows(L0_gamma), ALU.mult))
                    dve.wait_ge(beta_ready, 1)
                    link(nc.vector.tensor_tensor(x[:], x_beta[:], t[:], ALU.add))
                    statistics(dve, link, lambda c: x[:, c, :], var_ready, std_ready, 1)
                    normalize_relu(link, NORM_SCALE, True, scale_ready, h_ready)
                    dve.wait_ge(h_ready, 2)
                    split_table(link, h, parts)
                    first_window()

                @block.sync
                def _(sp):
                    sp.wait_ge(h_ready, 2)
                    sp.dma_start(table.rearrange("(p c) f -> p c f", c=C), h[:]).then_inc(stored, 16)
                    sp.wait_ge(stored, 16)

        l1_edges()

        def l1_tail(dve, link, k, projected, var_ready, std_ready, z_ready, tanh_done):
            for b in range(BANKS):
                dve.wait_ge(projected, b + 1)
                last = nc.vector.tensor_tensor(
                    in_banks(t[:])[:, b], banks(F)[:, b],
                    dis[:, b * PER_BANK:(b + 1) * PER_BANK].unsqueeze(2).to_broadcast([PN, PER_BANK, F]), ALU.mult)
            link(last)
            nc.vector.tensor_tensor(t[:], t[:], node_rows(L1_b[k]), ALU.add).then_inc(z_ready, 1)
            dve.wait_ge(tanh_done, 1)
            statistics(dve, link, lambda c: h[:, c, :], var_ready, std_ready, 0)
            normalize(link, lambda c: h[:, c, :], t)
            link(nc.vector.tensor_tensor(t[:], t[:], node_rows(L1_g_scaled if k == 0 else L1_g[1]), ALU.mult))

        with signals("s_proj", "s_steps", "s_var", "s_std", "s_h", "s_turned", "s_z", "s_tanh", "s_stored") as S:
            projected, steps, var_ready, std_ready, h_ready, turn_done, z_ready, tanh_done, stored = S
            with nc.Block() as block:
                @block.tensor
                def _(pe):
                    project(pe, aggT, F, W1[0], F, projected)
                    pe.wait_ge(h_ready, 1)
                    turn(pe, h, turn_done)

                @block.scalar
                def _(act):
                    act.wait_ge(z_ready, 1)
                    nc.scalar.activation(h[:], t[:], ACT.Tanh).then_inc(tanh_done, 1)
                    root(act, var_ready, std_ready, 0)
                    take_turned(act, aggT, turn_done)

                @block.vector
                def _(dve):
                    link = linker(dve, steps)
                    l1_tail(dve, link, 0, projected, var_ready, std_ready, z_ready, tanh_done)
                    link(nc.vector.tensor_tensor(t[:], t[:], node_rows(L1_be_scaled), ALU.add))
                    nc.vector.tensor_tensor(h[:], t[:], per_node(dis), ALU.mult).then_inc(h_ready, 1)
                    dve.wait_ge(h_ready, 1)
                    split_table(link, h, parts)
                    first_window()

                @block.sync
                def _(sp):
                    sp.wait_ge(h_ready, 1)
                    sp.dma_start(table.rearrange("(p c) f -> p c f", c=C), h[:]).then_inc(stored, 16)
                    sp.wait_ge(stored, 16)

        l1_edges()

        PRE_TILES = 8
        PRE_STEPS = [(k, min(PRE_TILES, C - k)) for k in range(0, C, PRE_TILES)]

        def take_products(engine, copy, pre_done, pre_taken, odd):
            for s, (c0, n) in enumerate(PRE_STEPS):
                engine.wait_ge(pre_done, s + 1)
                pairs = [(k, min(2, n - k)) for k in range(0, n, 2)][odd::2]
                for k, m in pairs:
                    last = copy(pre[:, c0 + k:c0 + k + m, :],
                                ps[0:PN, 4 * (s % 2) + k // 2, 0:m * 2 * F].rearrange("p (k f) -> p k f", k=m))
                if pairs:
                    last.then_inc(pre_taken, 1)
                else:
                    engine.sem_inc(pre_taken, 1)

        with signals("s_proj", "s_steps", "s_var", "s_std", "s_h", "s_turned", "s_z", "s_tanh", "s_feat", "s_pre",
                     "s_even", "s_odd", "s_beta", "s_scale", "s_stored") as S:
            (projected, steps, var_ready, std_ready, h_ready, turn_done, z_ready, tanh_done, feat_ready, pre_done,
             even_taken, odd_taken, beta_ready, scale_ready, stored) = S
            with nc.Block() as block:
                @block.tensor
                def _(pe):
                    project(pe, aggT, F, W1_scaled, F, projected)
                    pe.wait_ge(h_ready, 2)
                    turn(pe, h, turn_done)
                    pe.wait_ge(feat_ready, TBANKS)
                    tiles = by_tile(featT, F1)
                    for s, (c0, n) in enumerate(PRE_STEPS):
                        if s >= 2:
                            pe.wait_ge(even_taken, s - 1)
                            pe.wait_ge(odd_taken, s - 1)
                        for c in range(c0, c0 + n):
                            k = c - c0
                            mm = pe.matmul(ps[0:PN, 4 * (s % 2) + k // 2, (k % 2) * 2 * F:(k % 2 + 1) * 2 * F],
                                           tiles[:, c, :], W2in[:], start=True, stop=True)
                        mm.then_inc(pre_done, 1)

                @block.scalar
                def _(act):
                    act.wait_ge(z_ready, 1)
                    nc.scalar.activation(h[:], t[:], ACT.Tanh).then_inc(tanh_done, 1)
                    root(act, var_ready, std_ready, 0)
                    root(act, var_ready, std_ready, 1)
                    normalize_relu_act(act, scale_ready, h_ready)
                    take_turned(act, featT, turn_done, feat_ready)
                    take_products(act, nc.scalar.copy, pre_done, odd_taken, 1)

                @block.gpsimd
                def _(pool):
                    add_beta(L1_be[1], beta_ready)
                    pool.wait_ge(projected, BANKS)
                    nc.gpsimd.memset(aggT[:], 0.0)

                @block.vector
                def _(dve):
                    link = linker(dve, steps)
                    l1_tail(dve, link, 1, projected, var_ready, std_ready, z_ready, tanh_done)
                    dve.wait_ge(beta_ready, 1)
                    link(nc.vector.tensor_tensor(x[:], x_beta[:], t[:], ALU.add))
                    statistics(dve, link, lambda c: x[:, c, :], var_ready, std_ready, 1)
                    normalize_relu(link, 1.0, False, scale_ready, h_ready)
                    first_window()
                    take_products(dve, nc.vector.tensor_copy, pre_done, even_taken, 0)

                @block.sync
                def _(sp):
                    sp.wait_ge(even_taken, len(PRE_STEPS))
                    sp.wait_ge(odd_taken, len(PRE_STEPS))
                    sp.dma_start(table2.rearrange("(p c) f -> p c f", c=C), pre[:]).then_inc(stored, 16)
                    sp.wait_ge(stored, 16)

        edge_pass("L2")

        with signals("s_hid", "s_hidt", "s_proj", "s_steps", "s_var", "s_std", "s_h", "s_turned",
                     "s_feat", "s_pre", "s_gelu", "s_tab", "s_beta", "s_scale", "s_stored") as S:
            (hid_done, hid_taken, projected, steps, var_ready, std_ready, h_ready, turn_done,
             feat_ready, pre_done, gelu_done, table_ready, beta_ready, scale_ready, stored) = S
            with nc.Block() as block:
                @block.tensor
                def _(pe):
                    for n, (at, w) in enumerate(CHUNKS):
                        pe.matmul(ps[0:F, n, 0:w], W2u_x[:], featT[0:F, at:at + w], start=True, stop=False)
                        pe.matmul(ps[0:F, n, 0:w], W2agg[:], aggT[0:F1, at:at + w], start=False,
                                  stop=True).then_inc(hid_done, 1)
                    pe.wait_ge(hid_taken, len(CHUNKS))
                    project(pe, hidT, F1, W2u2, F, projected)
                    pe.wait_ge(h_ready, 2)
                    turn(pe, h, turn_done)
                    pe.wait_ge(feat_ready, TBANKS)
                    project(pe, featT, F1, W3pre, F, pre_done)

                @block.scalar
                def _(act):
                    for n, (at, w) in enumerate(CHUNKS):
                        act.wait_ge(hid_done, n + 1)
                        nc.scalar.activation(hidT[0:F, at:at + w], ps[0:F, n, 0:w], ACT.Gelu,
                                             bias=L2_ub1[:, 0:1]).then_inc(hid_taken, 1)
                    root(act, var_ready, std_ready, 0)
                    root(act, var_ready, std_ready, 1)
                    normalize_relu_act(act, scale_ready, h_ready)
                    take_turned(act, featT, turn_done, feat_ready)
                    for b in range(BANKS):
                        act.wait_ge(pre_done, b + 1)
                        nc.scalar.activation(in_banks(t[:])[:, b], banks(F)[:, b], ACT.Gelu).then_inc(gelu_done, 1)

                @block.vector
                def _(dve):
                    link = linker(dve, steps)
                    for b in range(BANKS):
                        dve.wait_ge(projected, b + 1)
                        last = nc.vector.tensor_tensor(in_banks(t[:])[:, b], banks(F)[:, b], in_banks(h[:])[:, b],
                                                       ALU.add)
                    link(last)
                    statistics(dve, link, lambda c: t[:, c, :], var_ready, std_ready, 0)
                    normalize(link, lambda c: t[:, c, :], t)
                    link(nc.vector.tensor_tensor(t[:], t[:], node_rows(L2_g), ALU.mult))
                    dve.wait_ge(beta_ready, 1)
                    link(nc.vector.tensor_tensor(x[:], x_beta[:], t[:], ALU.add))
                    statistics(dve, link, lambda c: x[:, c, :], var_ready, std_ready, 1)
                    normalize_relu(link, 1.0, False, scale_ready, h_ready)
                    first_window()
                    for b in range(BANKS):
                        dve.wait_ge(gelu_done, b + 1)
                        nc.vector.tensor_tensor(in_banks(t[:])[:, b], in_banks(t[:])[:, b], bank_rows(power[1]),
                                                ALU.mult).then_inc(table_ready, 1)
                    dve.wait_ge(table_ready, BANKS)
                    split_table(link, t, parts)

                @block.gpsimd
                def _(pool):
                    add_beta(L2_b, beta_ready)
                    pool.wait_ge(hid_done, len(CHUNKS))
                    nc.gpsimd.memset(aggT[:], 0.0)

                @block.sync
                def _(sp):
                    sp.wait_ge(table_ready, BANKS)
                    sp.dma_start(table.rearrange("(p c) f -> p c f", c=C), t[:]).then_inc(stored, 16)
                    sp.wait_ge(stored, 16)

        edge_pass("L3")

        with signals("s_sum", "s_hid", "s_hidt", "s_proj", "s_xt", "s_y", "s_xd", "s_steps", "s_out", "s_stored") as S:
            sum_ready, hid_done, hid_taken, projected, x_turned, y_ready, x_taken, steps, out_ready, stored = S
            with nc.Block() as block:
                @block.tensor
                def _(pe):
                    for n, (at, w) in enumerate(CHUNKS):
                        pe.wait_ge(sum_ready, n + 1)
                        pe.matmul(ps[0:F, n, 0:w], W3a[:], aggT[0:F, at:at + w], start=True,
                                  stop=True).then_inc(hid_done, 1)
                    pe.wait_ge(hid_taken, len(CHUNKS))
                    project(pe, hidT, F1, W3b, F, projected)
                    pe.wait_ge(y_ready, BANKS)
                    project(pe, aggT, F, ident, F, x_turned)

                @block.scalar
                def _(act):
                    for n, (at, w) in enumerate(CHUNKS):
                        act.wait_ge(hid_done, n + 1)
                        nc.scalar.activation(hidT[0:F, at:at + w], ps[0:F, n, 0:w], ACT.Gelu,
                                             bias=L3_b1[:, 0:1]).then_inc(hid_taken, 1)
                    for b in range(BANKS):
                        act.wait_ge(projected, b + 1)
                        nc.scalar.activation(in_banks(t[:])[:, b], banks(F)[:, b], ACT.Gelu).then_inc(y_ready, 1)

                @block.vector
                def _(dve):
                    link = linker(dve, steps)
                    for n, (at, w) in enumerate(CHUNKS):
                        nc.vector.scalar_tensor_tensor(
                            out=aggT[0:F, at:at + w], in0=aggT[0:F, at:at + w], scalar=unscale[1][:, 0:1],
                            in1=featT[0:F, at:at + w], op0=ALU.mult, op1=ALU.add).then_inc(sum_ready, 1)
                    for b in range(BANKS):
                        dve.wait_ge(y_ready, b + 1)
                        last = nc.vector.tensor_tensor(in_banks(x[:])[:, b], in_banks(x[:])[:, b], in_banks(t[:])[:, b],
                                                       ALU.add)
                    link(last)
                    for b in range(BANKS):
                        dve.wait_ge(x_turned, b + 1)
                        nc.vector.tensor_tensor(in_banks(x[:])[:, b], banks(F)[:, b], in_banks(x[:])[:, b],
                                                ALU.add).then_inc(out_ready, 1)

                @block.sync
                def _(sp):
                    sp.wait_ge(out_ready, BANKS)
                    sp.dma_start(out.rearrange("(p c) f -> p c f", c=C), x[:]).then_inc(stored, 16)
                    sp.wait_ge(stored, 16)


def kernel(**inputs):
    import numpy as _np
    import concourse.bacc as _bacc
    from concourse import mybir as _mybir
    from concourse.bass_utils import run_bass_kernel_spmd as _run

    arrays = {k: _np.asarray(v) for k, v in inputs.items()}
    n_edges = arrays["src"].shape[0]
    groups = group_count(n_edges)

    def padded(a, fill):
        full = _np.full((groups * GROUP,) + a.shape[1:], fill, a.dtype)
        full[:n_edges] = a
        return full

    arrays["src"] = padded(arrays["src"], 0).reshape(groups, P, J)
    arrays["src_tiles"] = arrays["src"].transpose(0, 2, 1).reshape(groups, GROUP)
    arrays["src_cols"] = arrays["src"].transpose(1, 0, 2).reshape(P, groups * J)
    for name, fill in (("dst", -1), ("edge_weight", 0)):
        arrays[name] = padded(arrays[name], fill).reshape(groups, P, J).transpose(1, 0, 2).reshape(P, groups * J)
    arrays["edge_attr_96"] = padded(arrays["edge_attr_96"], 0).reshape(groups, P, -1)
    a = padded(arrays["edge_attr_32"], 0)
    f = a.shape[1]
    q = P // f
    arrays["edge_attr_32"] = a.reshape(groups, P, J // q, q, f).transpose(0, 3, 4, 2, 1).reshape(groups, P, -1)

    nc = _bacc.Bacc("TRN2", target_bir_lowering=False, num_devices=1)
    feeds, D = {}, {}
    for name, a in arrays.items():
        a = _np.ascontiguousarray(a)
        feeds[f"in_{name}"] = a
        D[name] = nc.dram_tensor(f"in_{name}", a.shape, _mybir.dt.from_np(a.dtype), kind="ExternalInput").ap()
    out = nc.dram_tensor("out_x", inputs["x"].shape, F32, kind="ExternalOutput").ap()
    program(nc, D, out)
    r = _run(nc, [feeds], core_ids=[0])
    return r.results[0]["out_x"]
```
